# Optimizing a Trainium2 kernel written in Bass

```python
import numpy as np
import jax
import jax.numpy as jnp

def _softmax(x, axis=-1):
    return jax.nn.softmax(x, axis=axis)

def _gelu(x):
    return jax.nn.gelu(x, approximate=True)

def _silu(x):
    return jax.nn.silu(x)

def _sigmoid(x):
    return jax.nn.sigmoid(x)

def _layernorm(x, axis=-1, eps=1e-05):
    m = jnp.mean(x, axis=axis, keepdims=True)
    v = jnp.var(x, axis=axis, keepdims=True)
    return (x - m) / jnp.sqrt(v + eps)

def _scatter_add(tgt, idx, src, axis=0):
    return tgt.at[idx].add(src)

def _segment_sum(src, seg, n):
    return jax.ops.segment_sum(src, seg, n)
kernel_name = 'mk_cond_resid_d4_seqx_r4_459fa4'

def setup_inputs(seed: int=0):
    np.random.seed(seed)
    _w = jnp.asarray

    def _rec_inputs():
        import jax
        import jax.numpy as jnp
        _rk = jax.random.key(seed)
        x = -0.0003929 + 0.9999 * jax.random.normal(jax.random.fold_in(_rk, 1), (8, 256, 256), jnp.float32)
        _lenS = 256 - jax.random.randint(jax.random.fold_in(_rk, 7), (8,), 0, max(1, 256 // 4) + 1, jnp.int32)
        _lenS2 = 256 - jax.random.randint(jax.random.fold_in(_rk, 8), (8,), 0, max(1, 256 // 4) + 1, jnp.int32)
        itok_B_0_63 = jax.random.randint(jax.random.fold_in(_rk, 11), (8,), 0, 64, jnp.int32)
        itok_B_0_2 = jax.random.randint(jax.random.fold_in(_rk, 12), (8,), 0, 3, jnp.int32)
        itok_B_0_7 = jax.random.randint(jax.random.fold_in(_rk, 13), (8,), 0, 8, jnp.int32)
        itok_B_0_6 = jax.random.randint(jax.random.fold_in(_rk, 14), (8,), 0, 7, jnp.int32)
        return (x, itok_B_0_63, itok_B_0_2, itok_B_0_7, itok_B_0_6)
    x, itok_B_0_63, itok_B_0_2, itok_B_0_7, itok_B_0_6 = _rec_inputs()

    def _L0_cond_setup():
        import jax, jax.numpy as jnp
        import numpy as np
        NUM_CATEGORIES = 64
        INPUT_DIM = 256
        HIDDEN_DIM = 256
        B = 64
        S = 64
        key = jax.random.key(seed)
        kx, kc, kw = jax.random.split(key, 3)
        x = jax.random.normal(kx, (B, S, INPUT_DIM), dtype=jnp.float32)
        cat_ids = jax.random.randint(kc, (B,), 0, NUM_CATEGORIES, dtype=jnp.int32)
        W = 0.02 * jax.random.normal(kw, (NUM_CATEGORIES, INPUT_DIM, HIDDEN_DIM), dtype=jnp.float32)
        b = jnp.zeros((NUM_CATEGORIES, HIDDEN_DIM), dtype=jnp.float32)
        return {'x': x, 'cat_ids': cat_ids, 'W': W, 'b': b}
    _L0_cond_all = _L0_cond_setup()
    _L0_cond_in = {k: v for k, v in _L0_cond_all.items() if k in ('W', 'b')}
    del _L0_cond_all

    def _L1_cond_setup():
        import jax, jax.numpy as jnp
        import numpy as np
        NEG_INF = -1e+30
        key = jax.random.key(seed)
        k1, k2, k3, k4, k5 = jax.random.split(key, 5)
        B, S, D, A = (16, 256, 256, 64)
        hidden = jax.random.normal(k1, (B, S, D), dtype=jnp.float32)
        W1 = jax.random.normal(k2, (D, A), dtype=jnp.float32) / np.sqrt(D)
        b1 = jax.random.normal(k3, (A,), dtype=jnp.float32) * 0.01
        v = jax.random.normal(k4, (A,), dtype=jnp.float32) / np.sqrt(A)
        prompt_type_ids = jax.random.randint(k5, (B,), 0, 3, dtype=jnp.int32)
        return {'hidden': hidden, 'W1': W1, 'b1': b1, 'v': v, 'prompt_type_ids': prompt_type_ids}
    _L1_cond_all = _L1_cond_setup()
    _L1_cond_in = {k: v for k, v in _L1_cond_all.items() if k in ('W1', 'b1', 'v')}
    del _L1_cond_all

    def _L2_cond_setup():
        import jax, jax.numpy as jnp
        import numpy as np
        S, O, H = (8, 256, 256)
        B, N = (32, 128)
        key = jax.random.key(seed)
        k1, k2, k3, k4 = jax.random.split(key, 4)
        x = jax.random.normal(k1, (B, N, H), dtype=jnp.float32)
        subject_id = jax.random.randint(k2, (B,), 0, S)
        wbound = jnp.sqrt(2.0 / 6.0) * jnp.sqrt(3.0 / H)
        weight = jax.random.uniform(k3, (S, O, H), minval=-wbound, maxval=wbound, dtype=jnp.float32)
        bbound = 1.0 / jnp.sqrt(H)
        bias = jax.random.uniform(k4, (S, O), minval=-bbound, maxval=bbound, dtype=jnp.float32)
        return {'x': x, 'subject_id': subject_id, 'weight': weight, 'bias': bias}
    _L2_cond_all = _L2_cond_setup()
    _L2_cond_in = {k: v for k, v in _L2_cond_all.items() if k in ('weight', 'bias')}
    del _L2_cond_all

    def _L3_cond_setup():
        import jax, jax.numpy as jnp
        import numpy as np
        N_PROFILES = 8
        HIDDEN = 256
        BOTTLENECK = 128
        EPS = 1e-05
        key = jax.random.key(seed)
        ks = jax.random.split(key, 8)
        B, S, H, K, P = (16, 512, HIDDEN, BOTTLENECK, N_PROFILES)
        down_w = jax.random.normal(ks[0], (P, H, K), dtype=jnp.float32) * (1.0 / np.sqrt(H))
        down_b = jax.random.normal(ks[1], (P, K), dtype=jnp.float32) * 0.01
        up_w = jax.random.normal(ks[2], (P, K, H), dtype=jnp.float32) * (1.0 / np.sqrt(K))
        up_b = jax.random.normal(ks[3], (P, H), dtype=jnp.float32) * 0.01
        ln_g = jnp.ones((P, H), dtype=jnp.float32)
        ln_b = jnp.zeros((P, H), dtype=jnp.float32)
        hidden = jax.random.normal(ks[4], (B, S, H), dtype=jnp.float32)
        profile_ids = jax.random.randint(ks[5], (B,), 0, P)
        return {'hidden': hidden, 'profile_ids': profile_ids, 'down_w': down_w, 'down_b': down_b, 'up_w': up_w, 'up_b': up_b, 'ln_g': ln_g, 'ln_b': ln_b}
    _L3_cond_all = _L3_cond_setup()
    _L3_cond_in = {k: v for k, v in _L3_cond_all.items() if k in ('down_w', 'down_b', 'up_w', 'up_b', 'ln_g', 'ln_b')}
    del _L3_cond_all
    return {'x': x, 'itok_B_0_63': itok_B_0_63, 'itok_B_0_2': itok_B_0_2, 'itok_B_0_7': itok_B_0_7, 'itok_B_0_6': itok_B_0_6, 'L0_cond_W': _L0_cond_in['W'], 'L0_cond_b': _L0_cond_in['b'], 'L1_cond_W1': _L1_cond_in['W1'], 'L1_cond_b1': _L1_cond_in['b1'], 'L1_cond_v': _L1_cond_in['v'], 'L2_cond_weight': _L2_cond_in['weight'], 'L2_cond_bias': _L2_cond_in['bias'], 'L3_cond_down_w': _L3_cond_in['down_w'], 'L3_cond_down_b': _L3_cond_in['down_b'], 'L3_cond_up_w': _L3_cond_in['up_w'], 'L3_cond_up_b': _L3_cond_in['up_b'], 'L3_cond_ln_g': _L3_cond_in['ln_g'], 'L3_cond_ln_b': _L3_cond_in['ln_b']}

def reference(x, itok_B_0_63, itok_B_0_2, itok_B_0_7, itok_B_0_6, L0_cond_W, L0_cond_b, L1_cond_W1, L1_cond_b1, L1_cond_v, L2_cond_weight, L2_cond_bias, L3_cond_down_w, L3_cond_down_b, L3_cond_up_w, L3_cond_up_b, L3_cond_ln_g, L3_cond_ln_b):
    import jax
    import jax.numpy as jnp

    def _L0_cond_ref(x, cat_ids, W, b):
        import jax, jax.numpy as jnp
        import numpy as np
        NUM_CATEGORIES = 64
        INPUT_DIM = 256
        HIDDEN_DIM = 256
        B = 64
        S = 64
        selected_W = W[cat_ids]
        selected_b = b[cat_ids]
        out = jnp.einsum('bsd,bdh->bsh', x, selected_W) + selected_b[:, None, :]
        return out

    def _L1_cond_ref(hidden, W1, b1, v, prompt_type_ids):
        import jax, jax.numpy as jnp
        import numpy as np
        NEG_INF = -1e+30
        B, S, D = hidden.shape
        attn_in = jnp.tanh(jnp.einsum('bsd,da->bsa', hidden, W1) + b1)
        scores = jnp.einsum('bsa,a->bs', attn_in, v)
        idx = jnp.arange(S)
        j = idx[:, None]
        l = idx[None, :]
        prefix_m = l <= j
        postfix_m = l >= j
        cloze_m = l != j
        pt = prompt_type_ids[:, None, None]
        mask = jnp.where(pt == 0, prefix_m[None], jnp.where(pt == 1, postfix_m[None], cloze_m[None]))
        masked_scores = jnp.where(mask, scores[:, None, :], NEG_INF)
        p = jax.nn.softmax(masked_scores, axis=-1)
        cnt = jnp.sum(mask, axis=-1).astype(hidden.dtype)
        pooled = jnp.einsum('bjl,bld->bjd', p, hidden) / cnt[..., None]
        return pooled

    def _L2_cond_ref(x, subject_id, weight, bias):
        import jax, jax.numpy as jnp
        import numpy as np
        S, O, H = (8, 256, 256)
        B, N = (32, 128)
        W = weight[subject_id]
        b = bias[subject_id]
        y = jnp.einsum('bnh,boh->bno', x, W) + b[:, None, :]
        return y

    def _L3_cond_ref(hidden, profile_ids, down_w, down_b, up_w, up_b, ln_g, ln_b):
        import jax, jax.numpy as jnp
        import numpy as np
        N_PROFILES = 8
        HIDDEN = 256
        BOTTLENECK = 128
        EPS = 1e-05
        Wd = down_w[profile_ids]
        bd = down_b[profile_ids][:, None]
        Wu = up_w[profile_ids]
        bu = up_b[profile_ids][:, None]
        g = ln_g[profile_ids][:, None]
        b = ln_b[profile_ids][:, None]
        z = jax.nn.relu(jnp.einsum('bsh,bhk->bsk', hidden, Wd) + bd)
        y = hidden + jnp.einsum('bsk,bkh->bsh', z, Wu) + bu
        mu = jnp.mean(y, axis=-1, keepdims=True)
        var = jnp.mean(jnp.square(y - mu), axis=-1, keepdims=True)
        return (y - mu) * jax.lax.rsqrt(var + EPS) * g + b
    x = x + _L0_cond_ref(x, itok_B_0_63, L0_cond_W, L0_cond_b)
    x = x + _L1_cond_ref(x, L1_cond_W1, L1_cond_b1, L1_cond_v, itok_B_0_2)
    x = x + _L2_cond_ref(x, itok_B_0_7, L2_cond_weight, L2_cond_bias)
    x = x + _L3_cond_ref(x, itok_B_0_6, L3_cond_down_w, L3_cond_down_b, L3_cond_up_w, L3_cond_up_b, L3_cond_ln_g, L3_cond_ln_b)
    return x

_drawn_inputs = setup_inputs


def setup_inputs(seed=0):
    import zlib

    import numpy as np

    out = dict(_drawn_inputs(seed))
    spreads = {'L0_cond_b': (0.0, 0.1), 'L3_cond_ln_g': (1.0, 0.2), 'L3_cond_ln_b': (0.0, 0.1)}
    factors = {'L1_cond_W1': 5.679,
     'L1_cond_b1': 64.0,
     'L1_cond_v': 5.435,
     'L3_cond_down_b': 23.442,
     'L3_cond_up_b': 8.0}
    for name, (base, spread) in spreads.items():
        noise = np.random.default_rng([zlib.crc32(name.encode()), seed]).standard_normal(out[name].shape)
        drawn = base * np.exp(spread * noise) if base else spread * noise
        out[name] = jnp.asarray(drawn.astype(out[name].dtype))
    for name, factor in factors.items():
        out[name] = (out[name] * factor).astype(out[name].dtype)
    return out
```

```python
from contextlib import ExitStack

import concourse.bass as bass
from concourse import mybir

F32 = mybir.dt.float32
I32 = mybir.dt.int32
ALU = mybir.AluOpType
ACT = mybir.ActivationFunctionType

P = 128
BATCHES, SEQ, DIM = 8, 256, 256
CH = DIM // P
TB = SEQ // P
ATT = 64
BOT = 128
NTYPES = 3
ROW = CH * DIM
W0_COLS = ROW + CH
W2_COLS = ROW + CH
W3_COLS = CH * BOT + DIM + 1 + 3 * CH
MASKED = 1e30
HUGE = 3e38
EPS = 1e-5
STAGES = 4
STEPS = BATCHES + STAGES - 1
LOOP_FROM, LOOP_TO = 3, 7


def build(nc, xT, w0, w1, b1, v, w2, w3, ids, out):
    with ExitStack() as ctx:
        def sb(name, shape, dt=F32):
            return ctx.enter_context(nc.sbuf_tensor(name, shape, dt))

        def pair(name, shape, dt=F32):
            return [sb(f"{name}{i}", shape, dt) for i in range(2)]

        def bank(name):
            return ctx.enter_context(nc.psum_tensor(name, [P, 512], F32))

        def sem(name):
            return ctx.enter_context(nc.semaphore(name))

        ident = sb("ident", [P, P])
        ones = sb("ones", [P, P])
        masks = sb("masks", [P, NTYPES, TB * SEQ])
        counts = sb("counts", [P, NTYPES, TB])
        half_neg = sb("half_neg", [P, TB])
        w1_sb = sb("w1_sb", [P, CH, ATT])
        b1_sb = sb("b1_sb", [P, ATT])
        v_sb = sb("v_sb", [P, ATT])
        ids_sb = sb("ids_sb", [1, 4 * BATCHES], I32)
        x0_fm = pair("x0_fm", [P, CH, SEQ])
        w0_sb = pair("w0_sb", [P, W0_COLS])
        w2_sb = pair("w2_sb", [P, W2_COLS])
        w3_sb = pair("w3_sb", [P, W3_COLS])
        x1_fm = pair("x1_fm", [P, CH, SEQ])
        x1_tm = pair("x1_tm", [P, TB, DIM])
        pre = pair("pre", [P, TB, ATT])
        att = pair("att", [P, TB, ATT])
        attv = pair("attv", [P, TB, ATT])
        nscore = pair("nscore", [P, TB])
        mask_b = pair("mask_b", [P, TB * SEQ])
        count_b = pair("count_b", [P, TB])
        nmasked = pair("nmasked", [P, TB, SEQ])
        nmax = pair("nmax", [P, TB])
        prob = pair("prob", [P, TB, SEQ])
        psum_row = pair("psum_row", [P, TB])
        rcount = pair("rcount", [P, TB])
        rsum = pair("rsum", [P, TB])
        rdenom = pair("rdenom", [P, TB])
        prob_t = pair("prob_t", [P, TB, SEQ])
        x2_tm = pair("x2_tm", [P, TB, DIM])
        x2_fm = pair("x2_fm", [P, CH, SEQ])
        x3_fm = pair("x3_fm", [P, CH, SEQ])
        z_fm = pair("z_fm", [P, SEQ])
        y_fm = pair("y_fm", [P, CH, SEQ])
        stats = pair("stats", [P, TB, 6])
        meanvar = pair("meanvar", [P, TB, 2])
        veps = pair("veps", [P, TB])
        rstd = pair("rstd", [P, TB])
        nmean = pair("nmean", [P, TB])
        n_tm = pair("n_tm", [P, TB, DIM])
        scaled = pair("scaled", [P, CH, SEQ])
        out_fm = pair("out_fm", [P, CH, SEQ])

        ps_l0 = bank("ps_l0")
        ps_x1 = bank("ps_x1")
        ps_xp = bank("ps_xp")
        ps_upn = bank("ps_upn")
        ps_pl = bank("ps_pl")
        ps_y = bank("ps_y")
        ps_s = bank("ps_s")
        ps_dt = bank("ps_dt")
        ps_up = [ps_upn[:, 0:SEQ], ps_l0[:, 0:SEQ]]
        ps_l2 = [ps_pl[:, 0:SEQ], ps_x1[:, 0:SEQ]]

        ids_in = sem("ids_in")
        consts_in = sem("consts_in")
        x0_in = [sem(f"x0_in{i}") for i in range(2)]
        w0_in = [sem(f"w0_in{i}") for i in range(2)]
        w2_in = [sem(f"w2_in{i}") for i in range(2)]
        w3_in = [sem(f"w3_in{i}") for i in range(2)]
        stored = [sem(f"stored{i}") for i in range(2)]
        gp_own = sem("gp_own")
        ident_ready = sem("ident_ready")
        l0_done = sem("l0_done")
        down_done = sem("down_done")
        probt_done = sem("probt_done")
        up_done = sem("up_done")
        pool_done = sem("pool_done")
        x1t_done = sem("x1t_done")
        att_done = sem("att_done")
        x2t_done = sem("x2t_done")
        nt_done = sem("nt_done")
        yt_done = sem("yt_done")
        l2_done = sem("l2_done")
        score_done = sem("score_done")
        nmask_ready = sem("nmask_ready")
        x1fm_ready = sem("x1fm_ready")
        rcount_ready = sem("rcount_ready")
        rsum_ready = sem("rsum_ready")
        veps_ready = sem("veps_ready")
        rdenom_ready = sem("rdenom_ready")
        yfm_ready = sem("yfm_ready")
        x2tm_ready = sem("x2tm_ready")
        pre_ready = sem("pre_ready")
        nscore_ready = sem("nscore_ready")
        stats_ready = sem("stats_ready")
        meanvar_ready = sem("meanvar_ready")
        nmean_ready = sem("nmean_ready")
        x3fm_ready = sem("x3fm_ready")
        prob_ready = sem("prob_ready")
        z_ready = sem("z_ready")
        probt_ready = sem("probt_ready")
        x1tm_ready = sem("x1tm_ready")
        tanh_ready = sem("tanh_ready")
        x2fm_ready = sem("x2fm_ready")
        scaled_ready = sem("scaled_ready")
        ntm_ready = sem("ntm_ready")
        mask_ready = sem("mask_ready")
        rstd_ready = sem("rstd_ready")
        out_ready = sem("out_ready")

        def run(eng, step):
            for t in range(LOOP_FROM):
                step(0, t)
            with eng.Fori(0, (LOOP_TO - LOOP_FROM) // 2) as q:
                step(q, LOOP_FROM)
                step(q, LOOP_FROM + 1)
            for t in range(LOOP_TO, STEPS):
                step(0, t)

        def batch_of(q, r, stage):
            b = r - stage
            if isinstance(q, int) and not 0 <= b < BATCHES:
                return None
            return 2 * q + b, b % 2

        def upto(b, per_batch=1):
            return b * per_batch + per_batch

        def loads(q, r, stage, back=0):
            return (q + (r - stage) // 2 + 1 - back) * 16

        def settle(eng, loaded, value):
            eng.wait_ge(loaded, value)

        block = ctx.enter_context(nc.Block())

        @block.sync
        def _(sp):
            sp.dma_start(ids_sb[:, :], ids).then_inc(ids_in, 16)
            sp.wait_ge(ids_in, 16)

            def load_x_w0(q, r, wait=True):
                b, p = 2 * q + r, r % 2
                if wait:
                    sp.wait_ge(l0_done, upto(b - 2))
                    sp.wait_ge(x1fm_ready, upto(b - 2, CH))
                sp.dma_start(x0_fm[p][:, :, :], xT[bass.ds(b, 1), :, :, :].rearrange("o p c s -> (o p) c s")).then_inc(x0_in[p], 16)
                i = sp.value_load(ids_sb[0:1, bass.ds(b, 1)], min_val=0, max_val=w0.shape[0] - 1)
                sp.dma_start(w0_sb[p][:, :], w0[bass.ds(i, 1), :, :].rearrange("o p n -> (o p) n")).then_inc(w0_in[p], 16)

            def load_w2(q, r, wait=True):
                b, p = 2 * q + r, r % 2
                if wait:
                    sp.wait_ge(l2_done, upto(b - 2, CH))
                    sp.wait_ge(x3fm_ready, upto(b - 2, CH))
                i = sp.value_load(ids_sb[0:1, bass.ds(b + 2 * BATCHES, 1)], min_val=0, max_val=w2.shape[0] - 1)
                sp.dma_start(w2_sb[p][:, :], w2[bass.ds(i, 1), :, :].rearrange("o p n -> (o p) n")).then_inc(w2_in[p], 16)

            def load_w3(q, r, wait=True):
                b, p = 2 * q + r, r % 2
                if wait:
                    sp.wait_ge(scaled_ready, upto(b - 2))
                i = sp.value_load(ids_sb[0:1, bass.ds(b + 3 * BATCHES, 1)], min_val=0, max_val=w3.shape[0] - 1)
                sp.dma_start(w3_sb[p][:, :], w3[bass.ds(i, 1), :, :].rearrange("o p n -> (o p) n")).then_inc(w3_in[p], 16)

            load_x_w0(0, 0, wait=False)
            sp.dma_start(w1_sb[:, :, :], w1).then_inc(consts_in, 16)
            sp.dma_start(b1_sb[:, :], b1.to_broadcast([P, ATT])).then_inc(consts_in, 16)
            sp.dma_start(v_sb[:, :], v.to_broadcast([P, ATT])).then_inc(consts_in, 16)

            def step(q, r):
                looped = not isinstance(q, int)
                if looped or r + 1 < BATCHES:
                    load_x_w0(q, r + 1, wait=looped or r + 1 >= 2)
                if looped or r < BATCHES:
                    load_w2(q, r, wait=looped or r >= 2)
                if looped or 1 <= r <= BATCHES:
                    load_w3(q, r - 1, wait=looped or r - 1 >= 2)
                d = batch_of(q, r, 3)
                if d:
                    b, p = d
                    sp.wait_ge(out_ready, upto(b))
                    sp.dma_start(out[bass.ds(b, 1), :, :, :].rearrange("o p c s -> (o p) c s"), out_fm[p][:, :, :]).then_inc(stored[p], 16)

            run(sp, step)
            for p in range(2):
                sp.wait_ge(stored[p], 16 * BATCHES // 2)

        @block.tensor
        def _(pe):
            pe.wait_ge(ident_ready, 1)

            def score_layer(p, s):
                for k in range(CH):
                    mm = nc.tensor.matmul(ps_dt[:, s * ATT:(s + 1) * ATT], x1_fm[p][:, k, s * P:(s + 1) * P],
                                          w1_sb[:, k, :], start=(k == 0), stop=(k == CH - 1))
                return mm

            def step(q, r):
                A, B, C, D = (batch_of(q, r, s) for s in range(STAGES))
                if A:
                    b, p = A
                    pe.wait_ge(x0_in[p], loads(q, r, 0))
                    pe.wait_ge(w0_in[p], loads(q, r, 0))
                    for m in range(CH):
                        for k in range(CH):
                            mm = nc.tensor.matmul(ps_l0[:, m * SEQ:(m + 1) * SEQ], w0_sb[p][:, k * DIM + m * P:k * DIM + (m + 1) * P],
                                                  x0_fm[p][:, k, :], start=(k == 0), stop=(k == CH - 1))
                    mm.then_inc(l0_done, 1)
                if C:
                    b, p = C
                    pe.wait_ge(w3_in[p], loads(q, r, 2))
                    for k in range(CH):
                        pe.wait_ge(x3fm_ready, CH * b + k + 1)
                        mm = nc.tensor.matmul(ps_dt[:, 0:SEQ], w3_sb[p][:, k * BOT:(k + 1) * BOT], x3_fm[p][:, k, :],
                                              start=(k == 0), stop=(k == CH - 1))
                    mm.then_inc(down_done, 1)
                if B:
                    b, p = B
                    for j in range(TB):
                        pe.wait_ge(prob_ready, TB * b + j + 1)
                        for l in range(TB):
                            mm = nc.tensor.transpose(ps_xp[:, l * SEQ + j * P:l * SEQ + (j + 1) * P],
                                                     prob[p][:, j, l * P:(l + 1) * P], ident[:, :])
                    mm.then_inc(probt_done, 1)
                if D:
                    b, p = D
                    pe.wait_ge(ntm_ready, upto(b))
                    for s in range(TB):
                        for k in range(CH):
                            mm = nc.tensor.transpose(ps_y[:, k * SEQ + s * P:k * SEQ + (s + 1) * P],
                                                     n_tm[p][:, s, k * P:(k + 1) * P], ident[:, :])
                    mm.then_inc(nt_done, 1)
                if C:
                    b, p = C
                    pe.wait_ge(z_ready, upto(b))
                    if A:
                        pe.wait_ge(x1fm_ready, upto(A[0], CH))
                    for m in range(CH):
                        nc.tensor.matmul(ps_up[m], w3_sb[p][:, CH * BOT + m * P:CH * BOT + (m + 1) * P],
                                         z_fm[p][:, :], start=True, stop=True).then_inc(up_done, 1)
                if B:
                    b, p = B
                    pe.wait_ge(probt_ready, upto(b))
                    pe.wait_ge(x1tm_ready, upto(b))
                    for j in range(TB):
                        for l in range(TB):
                            mm = nc.tensor.matmul(ps_pl[:, j * DIM:(j + 1) * DIM], prob_t[p][:, l, j * P:(j + 1) * P],
                                                  x1_tm[p][:, l, :], start=(l == 0), stop=(l == TB - 1))
                    mm.then_inc(pool_done, 1)
                if A:
                    b, p = A
                    pe.wait_ge(x1fm_ready, upto(b, CH))
                    for k in range(CH):
                        for s in range(TB):
                            mm = nc.tensor.transpose(ps_x1[:, s * DIM + k * P:s * DIM + (k + 1) * P],
                                                     x1_fm[p][:, k, s * P:(s + 1) * P], ident[:, :])
                    mm.then_inc(x1t_done, 1)
                    if isinstance(q, int) and b == 0:
                        pe.wait_ge(consts_in, 48)
                    score_layer(p, 0)
                if B:
                    b, p = B
                    for s in range(TB):
                        pe.wait_ge(x2tm_ready, TB * b + s + 1)
                        for k in range(CH):
                            mm = nc.tensor.transpose(ps_xp[:, k * SEQ + s * P:k * SEQ + (s + 1) * P],
                                                     x2_tm[p][:, s, k * P:(k + 1) * P], ident[:, :])
                    mm.then_inc(x2t_done, 1)
                if A:
                    score_layer(A[1], 1).then_inc(att_done, 1)
                if C:
                    b, p = C
                    pe.wait_ge(yfm_ready, upto(b, CH))
                    if D:
                        pe.wait_ge(scaled_ready, upto(D[0]))
                    for s in range(TB):
                        for k in range(CH):
                            mm = nc.tensor.transpose(ps_y[:, s * DIM + k * P:s * DIM + (k + 1) * P],
                                                     y_fm[p][:, k, s * P:(s + 1) * P], ident[:, :])
                    mm.then_inc(yt_done, 1)
                if B:
                    b, p = B
                    pe.wait_ge(w2_in[p], loads(q, r, 1))
                    pe.wait_ge(x2fm_ready, upto(b))
                    if A:
                        pe.wait_ge(x1tm_ready, upto(A[0]))
                    for m in range(CH):
                        for k in range(CH):
                            mm = nc.tensor.matmul(ps_l2[m], w2_sb[p][:, k * DIM + m * P:k * DIM + (m + 1) * P],
                                                  x2_fm[p][:, k, :], start=(k == 0), stop=(k == CH - 1))
                        mm.then_inc(l2_done, 1)
                if A:
                    b, p = A
                    pe.wait_ge(nscore_ready, upto(b, TB))
                    for l in range(TB):
                        mm = nc.tensor.transpose(ps_s[:, l * P:(l + 1) * P], nscore[p][:, l:l + 1].to_broadcast([P, P]), ident[:, :])
                    mm.then_inc(score_done, 1)

            run(pe, step)

        @block.vector
        def _(dve):
            dve.wait_ge(consts_in, 48)

            def step(q, r):
                A, B, C, D = (batch_of(q, r, s) for s in range(STAGES))
                if B:
                    b, p = B
                    dve.wait_ge(mask_ready, upto(b))
                    dve.wait_ge(score_done, upto(b))
                    nc.vector.reciprocal(rcount[p][:, :], count_b[p][:, :]).then_inc(rcount_ready, 1)
                    for j in range(TB):
                        nc.vector.tensor_tensor_reduce(nmasked[p][:, j, :], ps_s[:, 0:SEQ], mask_b[p][:, j * SEQ:(j + 1) * SEQ],
                                                       1.0, HUGE, ALU.add, ALU.min, nmax[p][:, j:j + 1]).then_inc(nmask_ready, 1)
                if A:
                    b, p = A
                    dve.wait_ge(l0_done, upto(b))
                    for m in range(CH):
                        nc.vector.scalar_tensor_tensor(x1_fm[p][:, m, :], ps_l0[:, m * SEQ:(m + 1) * SEQ], w0_sb[p][:, ROW + m:ROW + m + 1],
                                                       x0_fm[p][:, m, :], ALU.add, ALU.add).then_inc(x1fm_ready, 1)
                if B:
                    b, p = B
                    dve.wait_ge(prob_ready, upto(b, TB))
                    nc.vector.reciprocal(rsum[p][:, :], psum_row[p][:, :]).then_inc(rsum_ready, 1)
                    dve.wait_ge(rsum_ready, upto(b))
                    dve.wait_ge(rcount_ready, upto(b))
                    nc.vector.tensor_tensor(rdenom[p][:, :], rsum[p][:, :], rcount[p][:, :], ALU.mult).then_inc(rdenom_ready, 1)
                if C:
                    b, p = C
                    c0 = CH * BOT + DIM + 1
                    for m in range(CH):
                        dve.wait_ge(up_done, CH * b + m + 1)
                        nc.vector.scalar_tensor_tensor(y_fm[p][:, m, :], ps_up[m], w3_sb[p][:, c0 + m:c0 + m + 1],
                                                       x3_fm[p][:, m, :], ALU.add, ALU.add).then_inc(yfm_ready, 1)
                if B:
                    b, p = B
                    dve.wait_ge(pool_done, upto(b))
                    dve.wait_ge(rdenom_ready, upto(b))
                    for s in range(TB):
                        nc.vector.scalar_tensor_tensor(x2_tm[p][:, s, :], ps_pl[:, s * DIM:(s + 1) * DIM], rdenom[p][:, s:s + 1],
                                                       x1_tm[p][:, s, :], ALU.mult, ALU.add).then_inc(x2tm_ready, 1)
                if A:
                    b, p = A
                    dve.wait_ge(att_done, upto(b))
                    nc.vector.tensor_tensor(pre[p][:, :, :], ps_dt[:, 0:TB * ATT].rearrange("p (s a) -> p s a", s=TB),
                                            b1_sb[:, :].rearrange("p (o a) -> p o a", o=1).to_broadcast([P, TB, ATT]), ALU.add).then_inc(pre_ready, 1)
                if C:
                    b, p = C
                    dve.wait_ge(yt_done, upto(b))
                    for s in range(TB):
                        nc.vector.bn_stats(stats[p][:, s, :], ps_y[:, s * DIM:(s + 1) * DIM]).then_inc(stats_ready, 1)
                if A:
                    b, p = A
                    settle(dve, consts_in, 48)
                    dve.wait_ge(tanh_ready, upto(b))
                    for s in range(TB):
                        nc.vector.tensor_tensor_reduce(attv[p][:, s, :], att[p][:, s, :], v_sb[:, :], -1.0, 0.0,
                                                       ALU.mult, ALU.add, nscore[p][:, s:s + 1]).then_inc(nscore_ready, 1)
                if C:
                    b, p = C
                    for s in range(TB):
                        settle(dve, consts_in, 48)
                        dve.wait_ge(stats_ready, TB * b + s + 1)
                        nc.vector.bn_aggr(meanvar[p][:, s, :], stats[p][:, s, :]).then_inc(meanvar_ready, 1)
                    dve.wait_ge(meanvar_ready, upto(b, TB))
                    nc.vector.tensor_scalar(veps[p][:, :], meanvar[p][:, :, 1], EPS, None, ALU.add).then_inc(veps_ready, 1)
                if B:
                    b, p = B
                    if not isinstance(q, int) or b >= 2:
                        dve.wait_ge(out_ready, upto(b - 2))
                    for m in range(CH):
                        dve.wait_ge(l2_done, CH * b + m + 1)
                        nc.vector.scalar_tensor_tensor(x3_fm[p][:, m, :], ps_l2[m], w2_sb[p][:, ROW + m:ROW + m + 1],
                                                       x2_fm[p][:, m, :], ALU.add, ALU.add).then_inc(x3fm_ready, 1)
                if C:
                    b, p = C
                    dve.wait_ge(rstd_ready, upto(b))
                    nc.vector.scalar_tensor_tensor(nmean[p][:, :], meanvar[p][:, :, 0], -1.0, rstd[p][:, :], ALU.mult, ALU.mult).then_inc(nmean_ready, 1)

            run(dve, step)

        @block.scalar
        def _(act):
            def step(q, r):
                A, B, C, D = (batch_of(q, r, s) for s in range(STAGES))
                if B:
                    b, p = B
                    for j in range(TB):
                        act.wait_ge(nmask_ready, TB * b + j + 1)
                        nc.scalar.activation(prob[p][:, j, :], nmasked[p][:, j, :], ACT.Exp, bias=nmax[p][:, j:j + 1], scale=-1.0,
                                             accum_out=psum_row[p][:, j:j + 1]).then_inc(prob_ready, 1)
                if C:
                    b, p = C
                    act.wait_ge(down_done, upto(b))
                    c0 = CH * BOT + DIM
                    nc.scalar.activation(z_fm[p][:, :], ps_dt[:, 0:SEQ], ACT.Relu, bias=w3_sb[p][:, c0:c0 + 1]).then_inc(z_ready, 1)
                if B:
                    b, p = B
                    act.wait_ge(probt_done, upto(b))
                    nc.scalar.copy(prob_t[p][:, :, :].rearrange("p l j -> p (l j)"), ps_xp[:, :]).then_inc(probt_ready, 1)
                if D:
                    b, p = D
                    act.wait_ge(nt_done, upto(b))
                    c0 = CH * BOT + DIM + 1 + CH
                    for m in range(CH):
                        a = nc.scalar.activation(scaled[p][:, m, :], ps_y[:, m * SEQ:(m + 1) * SEQ], ACT.Identity,
                                                 scale=w3_sb[p][:, c0 + m:c0 + m + 1], bias=w3_sb[p][:, c0 + CH + m:c0 + CH + m + 1])
                    a.then_inc(scaled_ready, 1)
                if A:
                    b, p = A
                    act.wait_ge(x1t_done, upto(b))
                    nc.scalar.copy(x1_tm[p][:, :, :].rearrange("p s d -> p (s d)"), ps_x1[:, :]).then_inc(x1tm_ready, 1)
                if B:
                    b, p = B
                    act.wait_ge(x2t_done, upto(b))
                    nc.scalar.copy(x2_fm[p][:, :, :].rearrange("p c s -> p (c s)"), ps_xp[:, :]).then_inc(x2fm_ready, 1)
                if A:
                    b, p = A
                    act.wait_ge(pre_ready, upto(b))
                    nc.scalar.activation(att[p][:, :, :], pre[p][:, :, :], ACT.Tanh).then_inc(tanh_ready, 1)
                if C:
                    b, p = C
                    act.wait_ge(nmean_ready, upto(b))
                    for s in range(TB):
                        a = nc.scalar.activation(n_tm[p][:, s, :], ps_y[:, s * DIM:(s + 1) * DIM], ACT.Identity,
                                                 scale=rstd[p][:, s:s + 1], bias=nmean[p][:, s:s + 1])
                    a.then_inc(ntm_ready, 1)

            run(act, step)

        @block.gpsimd
        def _(pool):
            own = 0

            def made(ins):
                nonlocal own
                own += 1
                ins.then_inc(gp_own, 1)
                pool.wait_ge(gp_own, own)

            made(nc.gpsimd.memset(ones[:, :], 1.0))
            nc.gpsimd.affine_select(out=ident[:, :], in_=ones[:, :], pattern=[[-1, P]], compare_op=ALU.is_equal,
                                    fill=0.0, base=0, channel_multiplier=1).then_inc(ident_ready, 1)
            made(nc.gpsimd.memset(masks[:, :, :], 0.0))
            nc.gpsimd.memset(half_neg[:, :], -0.5)
            for j in range(TB):
                part = [masks[:, k, j * SEQ:(j + 1) * SEQ] for k in range(NTYPES)]
                nc.gpsimd.affine_select(out=part[0], in_=part[0], pattern=[[-1, SEQ]], compare_op=ALU.is_ge,
                                        fill=MASKED, base=j * P, channel_multiplier=1)
                nc.gpsimd.affine_select(out=part[1], in_=part[1], pattern=[[1, SEQ]], compare_op=ALU.is_ge,
                                        fill=MASKED, base=-j * P, channel_multiplier=-1)
                nc.gpsimd.affine_select(out=part[2], in_=part[2], pattern=[[1, SEQ]], compare_op=ALU.not_equal,
                                        fill=MASKED, base=-j * P, channel_multiplier=-1)
                nc.gpsimd.iota(counts[:, 0, j:j + 1], pattern=[[1, 1]], base=j * P + 1, channel_multiplier=1,
                               allow_small_or_imprecise_dtypes=True)
                nc.gpsimd.iota(counts[:, 1, j:j + 1], pattern=[[1, 1]], base=SEQ - j * P, channel_multiplier=-1,
                               allow_small_or_imprecise_dtypes=True)
                last = nc.gpsimd.memset(counts[:, 2, j:j + 1], float(SEQ - 1))
            made(last)
            pool.wait_ge(ids_in, 16)

            def choose_mask(q, r):
                b, p = 2 * q + r, r % 2
                kind = pool.value_load(ids_sb[0:1, bass.ds(b + BATCHES, 1)], min_val=0, max_val=NTYPES - 1)
                nc.gpsimd.tensor_copy(mask_b[p][:, :], masks[:, bass.ds(kind, 1), :].rearrange("p o n -> p (o n)"))
                nc.gpsimd.tensor_copy(count_b[p][:, :], counts[:, bass.ds(kind, 1), :].rearrange("p o n -> p (o n)")).then_inc(mask_ready, 1)

            choose_mask(0, 0)

            def step(q, r):
                looped = not isinstance(q, int)
                A, B, C, D = (batch_of(q, r, s) for s in range(STAGES))
                if D:
                    b, p = D
                    pool.wait_ge(scaled_ready, upto(b))
                    if looped or b >= 2:
                        pool.wait_ge(stored[p], loads(q, r, 3, back=1))
                    nc.gpsimd.tensor_tensor(out_fm[p][:, :, :], scaled[p][:, :, :], x3_fm[p][:, :, :], ALU.add).then_inc(out_ready, 1)
                if C:
                    b, p = C
                    pool.wait_ge(veps_ready, upto(b))
                    nc.gpsimd.tensor_tensor(rstd[p][:, :], veps[p][:, :], half_neg[:, :], ALU.pow).then_inc(rstd_ready, 1)
                if looped or r + 1 < BATCHES:
                    if looped or r >= 1:
                        pool.wait_ge(rdenom_ready, upto(2 * q + r - 1))
                    choose_mask(q, r + 1)

            run(pool, step)


def kernel(x, itok_B_0_63, itok_B_0_2, itok_B_0_7, itok_B_0_6, L0_cond_W, L0_cond_b, L1_cond_W1, L1_cond_b1, L1_cond_v,
           L2_cond_weight, L2_cond_bias, L3_cond_down_w, L3_cond_down_b, L3_cond_up_w, L3_cond_up_b, L3_cond_ln_g, L3_cond_ln_b):
    import numpy as np
    import concourse.bacc as bacc
    from concourse.bass_utils import run_bass_kernel_spmd

    def rows(w):
        n, d, m = w.shape
        return w.reshape(n, d // P, P, m).transpose(0, 2, 1, 3).reshape(n, P, -1)

    a = {k: np.asarray(v) for k, v in dict(
        x=x, W0=L0_cond_W, b0=L0_cond_b, W1=L1_cond_W1, b1=L1_cond_b1, v=L1_cond_v, W2=L2_cond_weight, b2=L2_cond_bias,
        Wd=L3_cond_down_w, bd=L3_cond_down_b, Wu=L3_cond_up_w, bu=L3_cond_up_b, g=L3_cond_ln_g, b=L3_cond_ln_b).items()}
    host = {
        "xT": rows(a["x"].transpose(0, 2, 1)).reshape(BATCHES, P, CH, SEQ),
        "w0": np.concatenate([rows(a["W0"]), rows(a["b0"][:, :, None])], axis=2),
        "w1": rows(a["W1"][None]).reshape(P, CH, ATT),
        "b1": a["b1"].reshape(1, ATT),
        "v": a["v"].reshape(1, ATT),
        "w2": np.concatenate([rows(a["W2"].transpose(0, 2, 1)), rows(a["b2"][:, :, None])], axis=2),
        "w3": np.concatenate([rows(a["Wd"]), a["Wu"], a["bd"][:, :, None]]
                             + [rows(a[k][:, :, None]) for k in ("bu", "g", "b")], axis=2),
        "ids": np.concatenate([np.asarray(i) for i in (itok_B_0_63, itok_B_0_2, itok_B_0_7, itok_B_0_6)]).reshape(1, 4 * BATCHES),
    }
    nc = bacc.Bacc("TRN2", target_bir_lowering=False, num_devices=1)
    arrays, args = {}, []
    for name, arr in host.items():
        arr = np.ascontiguousarray(arr)
        arrays[f"{name}_dram"] = arr
        args.append(nc.dram_tensor(f"{name}_dram", arr.shape, mybir.dt.from_np(arr.dtype), kind="ExternalInput").ap())
    args.append(nc.dram_tensor("out_dram", (BATCHES, P, CH, SEQ), F32, kind="ExternalOutput").ap())
    build(nc, *args)
    r = run_bass_kernel_spmd(nc, [arrays], core_ids=[0])
    got = r.results[0]["out_dram"]
    return got.transpose(0, 3, 2, 1).reshape(BATCHES, SEQ, DIM)
```

```python
from contextlib import ExitStack

import concourse.bass as bass
from concourse import mybir

F32 = mybir.dt.float32
I32 = mybir.dt.int32
ALU = mybir.AluOpType
ACT = mybir.ActivationFunctionType
AX = mybir.AxisListType

P = 128
BATCHES, SEQ, DIM = 8, 256, 256
CH = DIM // P
TB = SEQ // P
ATT = 64
BOT = 128
NTYPES = 3
ROW = CH * DIM
W0_COLS = ROW + CH
W2_COLS = ROW + CH
W3_COLS = CH * BOT + DIM + 1 + 3 * CH
MASK_COLS = P + 2 * TB
MASKED = 1e30
HUGE = 3e38
EPS = 1e-5
WARMUP = 4
STAGES = 4
STEPS = BATCHES + STAGES - 1
LOOP_FROM, LOOP_TO = 3, 7


def build(nc, xT, w0, w1, b1, v, w2, w3, ids, out):
    with ExitStack() as ctx:
        def sb(name, shape, dt=F32):
            return ctx.enter_context(nc.sbuf_tensor(name, shape, dt))

        def pair(name, shape, dt=F32):
            return [sb(f"{name}{i}", shape, dt) for i in range(2)]

        def bank(name):
            return ctx.enter_context(nc.psum_tensor(name, [P, 512], F32))

        def sem(name):
            return ctx.enter_context(nc.semaphore(name))

        ident = sb("ident", [P, P])
        ones = sb("ones", [P, P])
        masks = sb("masks", [P, NTYPES, MASK_COLS])
        half_neg = sb("half_neg", [P, TB])
        w1_sb = sb("w1_sb", [P, CH, ATT])
        b1_sb = sb("b1_sb", [P, ATT])
        v_sb = sb("v_sb", [P, ATT])
        ids_sb = sb("ids_sb", [1, 4 * BATCHES], I32)
        x0_fm = pair("x0_fm", [P, CH, SEQ])
        w0_sb = pair("w0_sb", [P, W0_COLS])
        w2_sb = pair("w2_sb", [P, W2_COLS])
        w3_sb = pair("w3_sb", [P, W3_COLS])
        x1_fm = pair("x1_fm", [P, CH, SEQ])
        x1_tm = pair("x1_tm", [P, TB, DIM])
        pre = pair("pre", [P, TB, ATT])
        att = pair("att", [P, TB, ATT])
        attv = pair("attv", [P, TB, ATT])
        nscore = pair("nscore", [P, TB])
        mask_b = pair("mask_b", [P, MASK_COLS])
        rcount = pair("rcount", [P, TB])
        nbmax = pair("nbmax", [P, TB])
        nbmax_o = pair("nbmax_o", [P, TB])
        dkey = pair("dkey", [P, TB])
        nmasked = pair("nmasked", [P, TB, P])
        nmax = pair("nmax", [P, TB])
        dother = pair("dother", [P, TB])
        prob = pair("prob", [P, TB, P])
        psum_row = pair("psum_row", [P, TB])
        wother = pair("wother", [P, TB])
        rowsum = pair("rowsum", [P, TB])
        rsum = pair("rsum", [P, TB])
        rdenom = pair("rdenom", [P, TB])
        wother_n = pair("wother_n", [P, TB])
        prob_n = pair("prob_n", [P, TB, P])
        prob_t = pair("prob_t", [P, TB, P + 4])
        wother_all = pair("wother_all", [P, SEQ])
        x2_fm = pair("x2_fm", [P, CH, SEQ])
        x3_fm = pair("x3_fm", [P, CH, SEQ])
        z_fm = pair("z_fm", [P, SEQ])
        y_fm = pair("y_fm", [P, CH, SEQ])
        stats = pair("stats", [P, TB, 6])
        meanvar = pair("meanvar", [P, TB, 2])
        veps = pair("veps", [P, TB])
        rstd = pair("rstd", [P, TB])
        nmean = pair("nmean", [P, TB])
        n_tm = pair("n_tm", [P, TB, DIM])
        scaled = pair("scaled", [P, CH, SEQ])
        out_fm = pair("out_fm", [P, CH, SEQ])
        gb = pair("gb", [P, 2 * CH])
        x3_last = sb("x3_last", [P, CH, SEQ])
        x3b = sb("x3b", [P, CH, SEQ])
        centred = sb("centred", [P, TB, DIM])

        ps_l0 = bank("ps_l0")
        ps_x1 = bank("ps_x1")
        ps_xp = bank("ps_xp")
        ps_du = bank("ps_du")
        ps_pl = bank("ps_pl")
        ps_y = bank("ps_y")
        ps_s = bank("ps_s")
        ps_t = bank("ps_t")
        scores = ps_s[:, 0:SEQ]
        key_sums = ps_s[:, SEQ:SEQ + TB]
        down = ps_du[:, SEQ:2 * SEQ]
        ps_up = [ps_du[:, 0:SEQ], ps_x1[:, 0:SEQ]]
        ps_l2 = [ps_pl[:, 0:SEQ], ps_x1[:, 0:SEQ]]
        ps_l2_last = [ps_pl[:, 0:SEQ], ps_l0[:, 0:SEQ]]
        ps_l0_halves = [ps_l0[:, 0:SEQ], ps_l0[:, SEQ:2 * SEQ]]
        ps_l0_first = [ps_l0[:, 0:SEQ], ps_du[:, 0:SEQ]]
        ps_l0_second = [ps_pl[:, 0:SEQ], ps_xp[:, 0:SEQ]]
        ps_yt = [ps_y[:, s * DIM:(s + 1) * DIM] for s in range(TB)]
        ps_yt_last = [ps_t[:, 0:DIM], ps_l0[:, 0:DIM]]
        ps_n = [ps_y[:, 0:SEQ], ps_y[:, SEQ:2 * SEQ]]
        ps_n_last = [ps_xp[:, 0:SEQ], ps_s[:, 0:SEQ]]
        ps_pool = [x[:, :].rearrange("p (b n) -> p b n", b=TB) for x in (ps_pl, ps_t)]

        ids_in = sem("ids_in")
        consts_in = sem("consts_in")
        x0_in = [sem(f"x0_in{i}") for i in range(2)]
        w0_in = [sem(f"w0_in{i}") for i in range(2)]
        w2_in = [sem(f"w2_in{i}") for i in range(2)]
        w3_in = [sem(f"w3_in{i}") for i in range(2)]
        stored = [sem(f"stored{i}") for i in range(2)]
        gp_own = sem("gp_own")
        ident_ready = sem("ident_ready")
        l0_done = sem("l0_done")
        down_done = sem("down_done")
        probt_done = sem("probt_done")
        up_done = sem("up_done")
        pool_done = sem("pool_done")
        ksum_done = sem("ksum_done")
        x1t_done = sem("x1t_done")
        att_done = sem("att_done")
        nt_done = sem("nt_done")
        yt_done = sem("yt_done")
        l2_done = sem("l2_done")
        score_done = sem("score_done")
        nbmax_ready = sem("nbmax_ready")
        nbmax_o_ready = sem("nbmax_o_ready")
        dkey_ready = sem("dkey_ready")
        nmask_ready = sem("nmask_ready")
        dother_ready = sem("dother_ready")
        rowsum_ready = sem("rowsum_ready")
        probn_ready = sem("probn_ready")
        wothern_ready = sem("wothern_ready")
        x1fm_ready = sem("x1fm_ready")
        rcount_ready = sem("rcount_ready")
        rsum_ready = sem("rsum_ready")
        veps_ready = sem("veps_ready")
        rdenom_ready = sem("rdenom_ready")
        yfm_ready = sem("yfm_ready")
        x2fm_ready = sem("x2fm_ready")
        pre_ready = sem("pre_ready")
        nscore_ready = sem("nscore_ready")
        stats_ready = sem("stats_ready")
        meanvar_ready = sem("meanvar_ready")
        nmean_ready = sem("nmean_ready")
        x3fm_ready = sem("x3fm_ready")
        gb_ready = sem("gb_ready")
        x3b_ready = sem("x3b_ready")
        centred_ready = sem("centred_ready")
        last_n_ready = sem("last_n_ready")
        last_out_ready = sem("last_out_ready")
        ekey_ready = sem("ekey_ready")
        wother_ready = sem("wother_ready")
        prob_ready = sem("prob_ready")
        z_ready = sem("z_ready")
        probt_ready = sem("probt_ready")
        wall_ready = sem("wall_ready")
        x1tm_ready = sem("x1tm_ready")
        tanh_ready = sem("tanh_ready")
        scaled_ready = sem("scaled_ready")
        ntm_ready = sem("ntm_ready")
        mask_ready = sem("mask_ready")
        rstd_ready = sem("rstd_ready")
        out_ready = sem("out_ready")

        def run(eng, step):
            step(0, LOOP_FROM - 1)
            with eng.Fori(0, (LOOP_TO - LOOP_FROM) // 2) as q:
                step(q, LOOP_FROM)
                step(q, LOOP_FROM + 1)
            step(0, LOOP_TO)

        def batch(q, r):
            if isinstance(q, int) and not 0 <= 2 * q + r < BATCHES:
                return None
            return 2 * q + r, r % 2, q + r // 2

        def upto(b, per_batch=1):
            return b * per_batch + per_batch

        def x3_of(X):
            return x3_last if isinstance(X[0], int) and X[0] == BATCHES - 1 else x3_fm[X[1]]

        def in_step(q, r):
            return [batch(q, r - s) for s in range(STAGES)] + [batch(q, r + 1)]

        HEAD = [batch(0, b) for b in range(3)]
        TAIL = [batch(0, b) for b in range(BATCHES - 3, BATCHES)]

        block = ctx.enter_context(nc.Block())

        @block.sync
        def _(sp):
            def row(table, b, field, n):
                return sp.value_load(table[0:1, bass.ds(b + field * BATCHES, 1)], min_val=0, max_val=n - 1)

            def load_x(X):
                b, p, n = X
                sp.dma_start(x0_fm[p][:, :, :], xT[bass.ds(b, 1), :, :, :].rearrange("o p c s -> (o p) c s")).then_inc(x0_in[p], 16)

            def load_w0(X, table):
                b, p, n = X
                i = row(table, b, 0, w0.shape[0])
                sp.dma_start(w0_sb[p][:, :], w0[bass.ds(i, 1), :, :].rearrange("o p n -> (o p) n")).then_inc(w0_in[p], 16)

            def load_x_w0(X, early=False):
                b, p, n = X
                if not early:
                    sp.wait_ge(l0_done, upto(b - 2, CH))
                    sp.wait_ge(x1fm_ready, upto(b - 2, CH))
                load_x(X)
                load_w0(X, ids if early else ids_sb)

            def load_w2(X, early=False):
                b, p, n = X
                if not early:
                    sp.wait_ge(l2_done, upto(b - 2, CH))
                    sp.wait_ge(x3fm_ready, upto(b - 2, CH))
                i = row(ids if early else ids_sb, b, 2, w2.shape[0])
                sp.dma_start(w2_sb[p][:, :], w2[bass.ds(i, 1), :, :].rearrange("o p n -> (o p) n")).then_inc(w2_in[p], 16)

            def load_w3(X, early=False):
                b, p, n = X
                if not early:
                    sp.wait_ge(yfm_ready, upto(b - 2, CH))
                i = row(ids if early else ids_sb, b, 3, w3.shape[0])
                sp.dma_start(w3_sb[p][:, :], w3[bass.ds(i, 1), :, :].rearrange("o p n -> (o p) n")).then_inc(w3_in[p], 16)

            def store(X):
                b, p, n = X
                sp.wait_ge(out_ready, upto(b, CH))
                sp.dma_start(out[bass.ds(b, 1), :, :, :].rearrange("o p c s -> (o p) c s"), out_fm[p][:, :, :]).then_inc(stored[p], 16)

            b0, b1_, b2 = HEAD
            load_w0(b0, ids)
            load_x_w0(b1_, early=True)
            load_w2(b0, early=True)
            sp.wait_ge(ids_in, 16)
            load_x_w0(b2)
            load_w2(b1_, early=True)
            load_w3(b0, early=True)

            def step(q, r):
                A, B, C, D, N = in_step(q, r)
                if N:
                    load_x_w0(N)
                load_w2(A)
                load_w3(B, early=isinstance(q, int) and B[0] < 2)
                if D:
                    store(D)

            run(sp, step)
            t5, t6, t7 = TAIL
            load_w3(t7)
            store(t5)
            store(t6)
            b, p, n = t7
            for m in range(CH):
                sp.wait_ge(last_out_ready, m + 1)
                sp.dma_start(out[b, :, m, :], out_fm[p][:, m, :]).then_inc(stored[p], 16)
            sp.wait_ge(stored[1 - p], 16 * (BATCHES // 2))
            sp.wait_ge(stored[p], 16 * (BATCHES // 2 - 1 + CH))

        @block.tensor
        def _(pe):
            def l0_half(X, m, banks=ps_l0_halves):
                b, p, n = X
                if m == 0:
                    pe.wait_ge(x0_in[p], (n + 1) * 16)
                    pe.wait_ge(w0_in[p], (n + 1) * 16)
                elif banks is ps_l0_halves:
                    pe.wait_ge(x1fm_ready, CH * b + 1)
                for k in range(CH):
                    mm = nc.tensor.matmul(banks[m], w0_sb[p][:, k * DIM + m * P:k * DIM + (m + 1) * P],
                                          x0_fm[p][:, k, :], start=(k == 0), stop=(k == CH - 1))
                mm.then_inc(l0_done, 1)

            def x1_to_tm(X):
                b, p, n = X
                pe.wait_ge(x1fm_ready, upto(b, CH))
                for k in range(CH):
                    for s in range(TB):
                        mm = nc.tensor.transpose(ps_x1[:, s * DIM + k * P:s * DIM + (k + 1) * P],
                                                 x1_fm[p][:, k, s * P:(s + 1) * P], ident[:, :])
                mm.then_inc(x1t_done, 1)

            def score_layer(X):
                b, p, n = X
                pe.wait_ge(x1fm_ready, upto(b, CH))
                for s in range(TB):
                    for k in range(CH):
                        mm = nc.tensor.matmul(ps_t[:, s * ATT:(s + 1) * ATT], x1_fm[p][:, k, s * P:(s + 1) * P],
                                              w1_sb[:, k, :], start=(k == 0), stop=(k == CH - 1))
                mm.then_inc(att_done, 1)

            def score_rows(X):
                b, p, n = X
                pe.wait_ge(nscore_ready, upto(b, TB))
                for l in range(TB):
                    mm = nc.tensor.transpose(scores[:, l * P:(l + 1) * P], nscore[p][:, l:l + 1].to_broadcast([P, P]), ident[:, :])
                mm.then_inc(score_done, 1)

            def key_sum_rows(X):
                b, p, n = X
                pe.wait_ge(ekey_ready, upto(b))
                pe.wait_ge(nmask_ready, upto(b, TB))
                nc.tensor.matmul(key_sums, ones[:, :], prob_t[p][:, :, P], start=True, stop=True).then_inc(ksum_done, 1)

            def transpose_probs(X):
                b, p, n = X
                pe.wait_ge(wothern_ready, upto(b))
                for j in range(TB):
                    nc.tensor.transpose(ps_xp[:, SEQ + j * P:SEQ + (j + 1) * P], wother_n[p][:, j:j + 1].to_broadcast([P, P]), ident[:, :])
                pe.wait_ge(probn_ready, upto(b, TB))
                for j in range(TB):
                    mm = nc.tensor.transpose(ps_xp[:, j * P:(j + 1) * P], prob_n[p][:, j, :], ident[:, :])
                mm.then_inc(probt_done, 1)

            def pool_half(X, m):
                b, p, n = X
                pe.wait_ge(probt_ready, upto(b))
                for j in range(TB):
                    mm = nc.tensor.matmul(ps_pool[m][:, j, 0:P + 1], x1_tm[p][:, j, m * P:(m + 1) * P],
                                          prob_t[p][:, j, 0:P + 1], start=True, stop=True)
                mm.then_inc(pool_done, 1)

            def l2(X, banks):
                b, p, n = X
                pe.wait_ge(w2_in[p], (n + 1) * 16)
                for k in range(CH):
                    pe.wait_ge(x2fm_ready, TB * CH * b + TB * (k + 1))
                    for m in range(CH):
                        mm = nc.tensor.matmul(banks[m], w2_sb[p][:, k * DIM + m * P:k * DIM + (m + 1) * P],
                                              x2_fm[p][:, k, :], start=(k == 0), stop=(k == CH - 1))
                        if k == CH - 1:
                            mm.then_inc(l2_done, 1)

            def adapter_down(X):
                b, p, n = X
                pe.wait_ge(w3_in[p], (n + 1) * 16)
                for k in range(CH):
                    pe.wait_ge(x3fm_ready, CH * b + k + 1)
                    mm = nc.tensor.matmul(down, w3_sb[p][:, k * BOT:(k + 1) * BOT], x3_of(X)[:, k, :],
                                          start=(k == 0), stop=(k == CH - 1))
                mm.then_inc(down_done, 1)

            def adapter_up(X, x1_in_bank=None):
                b, p, n = X
                pe.wait_ge(z_ready, upto(b))
                for m in range(CH):
                    if m == 1 and x1_in_bank:
                        pe.wait_ge(x1tm_ready, upto(x1_in_bank[0]))
                    nc.tensor.matmul(ps_up[m], w3_sb[p][:, CH * BOT + m * P:CH * BOT + (m + 1) * P],
                                     z_fm[p][:, :], start=True, stop=True).then_inc(up_done, 1)

            def y_to_tm(X, blocks):
                b, p, n = X
                for k in range(CH):
                    pe.wait_ge(yfm_ready, CH * b + k + 1)
                    for s in range(TB):
                        mm = nc.tensor.transpose(blocks[s][:, k * P:(k + 1) * P], y_fm[p][:, k, s * P:(s + 1) * P], ident[:, :])
                        if k == CH - 1:
                            mm.then_inc(yt_done, 1)

            def n_to_fm(X, chunks):
                b, p, n = X
                for k in range(CH):
                    for s in range(TB):
                        mm = nc.tensor.transpose(chunks[k][:, s * P:(s + 1) * P], n_tm[p][:, s, k * P:(k + 1) * P], ident[:, :])
                    mm.then_inc(nt_done, 1)

            pe.wait_ge(ident_ready, 1)
            for _ in range(WARMUP):
                nc.tensor.matmul(ps_y[:, 0:2 * P], ident[:, :], ident[:, :].rearrange("p (o n) -> p o n", o=1).to_broadcast([P, 2, P]),
                                 start=True, stop=True)
            b0, b1_, b2 = HEAD
            l0_half(b0, 0, ps_l0_first)
            l0_half(b0, 1, ps_l0_first)
            pe.wait_ge(consts_in, 48)
            score_layer(b0)
            x1_to_tm(b0)
            l0_half(b1_, 0, ps_l0_second)
            score_rows(b0)
            l0_half(b1_, 1, ps_l0_second)
            key_sum_rows(b0)
            l0_half(b2, 0)
            x1_to_tm(b1_)
            score_layer(b1_)
            transpose_probs(b0)
            pool_half(b0, 0)
            score_rows(b1_)
            pool_half(b0, 1)
            pe.wait_ge(x1tm_ready, upto(1))
            l2(b0, ps_l2)

            def step(q, r):
                A, B, C, D, N = in_step(q, r)
                key_sum_rows(B)
                l0_half(A, 1)
                adapter_down(C)
                x1_to_tm(A)
                score_layer(A)
                adapter_up(C, x1_in_bank=A)
                transpose_probs(B)
                if D:
                    pe.wait_ge(ntm_ready, upto(D[0]))
                    n_to_fm(D, ps_n)
                if N:
                    l0_half(N, 0)
                pool_half(B, 0)
                score_rows(A)
                pool_half(B, 1)
                if D:
                    pe.wait_ge(scaled_ready, upto(D[0], CH))
                y_to_tm(C, ps_yt)
                l2(B, ps_l2)

            run(pe, step)
            t5, t6, t7 = TAIL
            key_sum_rows(t7)
            adapter_down(t6)
            transpose_probs(t7)
            pool_half(t7, 0)
            pool_half(t7, 1)
            adapter_up(t6)
            l2(t7, ps_l2_last)
            pe.wait_ge(ntm_ready, upto(t5[0]))
            n_to_fm(t5, ps_n_last)
            adapter_down(t7)
            y_to_tm(t6, ps_yt)
            adapter_up(t7)
            y_to_tm(t7, ps_yt_last)
            pe.wait_ge(ntm_ready, upto(t6[0]))
            pe.wait_ge(scaled_ready, upto(t5[0], CH))
            n_to_fm(t6, ps_n_last)
            pe.wait_ge(ntm_ready, upto(t7[0]))
            pe.wait_ge(last_n_ready, 1)
            pe.wait_ge(scaled_ready, upto(t6[0], CH))
            n_to_fm(t7, ps_n_last)

        @block.vector
        def _(dve):
            def x1_half(X, m, banks=ps_l0_halves):
                b, p, n = X
                dve.wait_ge(l0_done, CH * b + m + 1)
                nc.vector.scalar_tensor_tensor(x1_fm[p][:, m, :], banks[m], w0_sb[p][:, ROW + m:ROW + m + 1],
                                               x0_fm[p][:, m, :], ALU.add, ALU.add).then_inc(x1fm_ready, 1)

            def score_bias(X):
                b, p, n = X
                dve.wait_ge(att_done, upto(b))
                nc.vector.tensor_tensor(pre[p][:, :, :], ps_t[:, 0:TB * ATT].rearrange("p (s a) -> p s a", s=TB),
                                        b1_sb[:, :].rearrange("p (o a) -> p o a", o=1).to_broadcast([P, TB, ATT]), ALU.add).then_inc(pre_ready, 1)

            def score_sums(X):
                b, p, n = X
                dve.wait_ge(consts_in, 48)
                dve.wait_ge(tanh_ready, upto(b))
                for s in range(TB):
                    nc.vector.tensor_tensor_reduce(attv[p][:, s, :], att[p][:, s, :], v_sb[:, :], -1.0, 0.0,
                                                   ALU.mult, ALU.add, nscore[p][:, s:s + 1]).then_inc(nscore_ready, 1)

            def block_maxima(X):
                b, p, n = X
                dve.wait_ge(mask_ready, upto(b))
                dve.wait_ge(score_done, upto(b))
                nc.vector.reciprocal(rcount[p][:, :], mask_b[p][:, P + TB:P + 2 * TB]).then_inc(rcount_ready, 1)
                nc.vector.tensor_reduce(nbmax[p][:, :], scores.rearrange("p (b l) -> p b l", b=TB), AX.X, ALU.min).then_inc(nbmax_ready, 1)

            def other_maxima(X):
                b, p, n = X
                dve.wait_ge(nbmax_ready, upto(b))
                for j in range(TB):
                    nc.vector.tensor_tensor(nbmax_o[p][:, j:j + 1], nbmax[p][:, 1 - j:2 - j], mask_b[p][:, P + j:P + j + 1], ALU.add).then_inc(nbmax_o_ready, 1)
                dve.wait_ge(nbmax_o_ready, upto(b, TB))
                nc.vector.tensor_tensor(dkey[p][:, :], nbmax[p][:, :], nscore[p][:, :], ALU.subtract).then_inc(dkey_ready, 1)

            def row_maxima(X):
                b, p, n = X
                for j in range(TB):
                    nc.vector.tensor_tensor_reduce(nmasked[p][:, j, :], scores[:, j * P:(j + 1) * P], mask_b[p][:, 0:P],
                                                   1.0, nbmax_o[p][:, j:j + 1], ALU.add, ALU.min, nmax[p][:, j:j + 1]).then_inc(nmask_ready, 1)
                dve.wait_ge(nmask_ready, upto(b, TB))
                nc.vector.tensor_tensor(dother[p][:, :], nmax[p][:, :], nbmax_o[p][:, :], ALU.subtract).then_inc(dother_ready, 1)

            def row_sums(X):
                b, p, n = X
                dve.wait_ge(prob_ready, upto(b, TB))
                dve.wait_ge(wother_ready, upto(b))
                dve.wait_ge(ksum_done, upto(b))
                for j in range(TB):
                    nc.vector.scalar_tensor_tensor(rowsum[p][:, j:j + 1], wother[p][:, j:j + 1], key_sums[:, 1 - j:2 - j],
                                                   psum_row[p][:, j:j + 1], ALU.mult, ALU.add).then_inc(rowsum_ready, 1)

            def row_sums_inverse(X):
                b, p, n = X
                dve.wait_ge(rowsum_ready, upto(b, TB))
                nc.vector.reciprocal(rsum[p][:, :], rowsum[p][:, :]).then_inc(rsum_ready, 1)

            def row_denominators(X):
                b, p, n = X
                dve.wait_ge(rsum_ready, upto(b))
                dve.wait_ge(rcount_ready, upto(b))
                nc.vector.tensor_tensor(rdenom[p][:, :], rsum[p][:, :], rcount[p][:, :], ALU.mult).then_inc(rdenom_ready, 1)

            def normalise(X):
                b, p, n = X
                dve.wait_ge(rdenom_ready, upto(b))
                nc.vector.tensor_tensor(wother_n[p][:, :], wother[p][:, :], rdenom[p][:, :], ALU.mult).then_inc(wothern_ready, 1)
                for j in range(TB):
                    nc.vector.scalar_tensor_tensor(prob_n[p][:, j, :], prob[p][:, j, :], rdenom[p][:, j:j + 1], ident[:, :],
                                                   ALU.mult, ALU.add).then_inc(probn_ready, 1)

            def x2_half(X, m):
                b, p, n = X
                if m == 0:
                    dve.wait_ge(wall_ready, upto(b))
                dve.wait_ge(pool_done, CH * b + m + 1)
                for j in range(TB):
                    nc.vector.scalar_tensor_tensor(x2_fm[p][:, m, j * P:(j + 1) * P], wother_all[p][:, j * P:(j + 1) * P],
                                                   ps_pool[m][:, 1 - j, P:P + 1], ps_pool[m][:, j, 0:P],
                                                   ALU.mult, ALU.add).then_inc(x2fm_ready, 1)

            def x3_half(X, m, banks=ps_l2):
                b, p, n = X
                dve.wait_ge(l2_done, CH * b + m + 1)
                nc.vector.scalar_tensor_tensor(x3_of(X)[:, m, :], banks[m], w2_sb[p][:, ROW + m:ROW + m + 1],
                                               x2_fm[p][:, m, :], ALU.add, ALU.add).then_inc(x3fm_ready, 1)

            def y_half(X, m):
                b, p, n = X
                c = CH * BOT + DIM + 1 + m
                dve.wait_ge(up_done, CH * b + m + 1)
                nc.vector.scalar_tensor_tensor(y_fm[p][:, m, :], ps_up[m], w3_sb[p][:, c:c + 1],
                                               x3_of(X)[:, m, :], ALU.add, ALU.add).then_inc(yfm_ready, 1)

            def keep_scale(X):
                b, p, n = X
                c = CH * BOT + DIM + 1 + CH
                nc.vector.tensor_copy(gb[p][:, :], w3_sb[p][:, c:c + 2 * CH]).then_inc(gb_ready, 1)

            def y_stats(X, blocks):
                b, p, n = X
                if blocks is ps_yt:
                    dve.wait_ge(yt_done, upto(b, TB))
                for s in range(TB):
                    if blocks is not ps_yt:
                        dve.wait_ge(yt_done, TB * b + s + 1)
                    nc.vector.bn_stats(stats[p][:, s, :], blocks[s]).then_inc(stats_ready, 1)

            def y_mean_var(X):
                b, p, n = X
                for s in range(TB):
                    nc.vector.bn_aggr(meanvar[p][:, s, :], stats[p][:, s, :]).then_inc(meanvar_ready, 1)

            def y_var_eps(X):
                b, p, n = X
                dve.wait_ge(meanvar_ready, upto(b, TB))
                nc.vector.tensor_scalar(veps[p][:, :], meanvar[p][:, :, 1], EPS, None, ALU.add).then_inc(veps_ready, 1)

            def y_shift(X):
                b, p, n = X
                dve.wait_ge(rstd_ready, upto(b))
                nc.vector.scalar_tensor_tensor(nmean[p][:, :], meanvar[p][:, :, 0], -1.0, rstd[p][:, :], ALU.mult, ALU.mult).then_inc(nmean_ready, 1)

            dve.wait_ge(consts_in, 48)
            dve.wait_ge(ident_ready, 1)
            b0, b1_, b2 = HEAD
            x1_half(b0, 0, ps_l0_first)
            x1_half(b0, 1, ps_l0_first)
            score_bias(b0)
            score_sums(b0)
            x1_half(b1_, 0, ps_l0_second)
            block_maxima(b0)
            other_maxima(b0)
            row_maxima(b0)
            x1_half(b1_, 1, ps_l0_second)
            row_sums(b0)
            row_sums_inverse(b0)
            row_denominators(b0)
            normalise(b0)
            score_bias(b1_)
            score_sums(b1_)
            x1_half(b2, 0)
            x2_half(b0, 0)
            block_maxima(b1_)
            x2_half(b0, 1)
            other_maxima(b1_)
            row_maxima(b1_)

            def step_until_y(q, r):
                A, B, C, D, N = in_step(q, r)
                dve.wait_ge(mask_ready, upto(A[0]))
                x3_half(C, 0)
                x3_half(C, 1)
                if D:
                    y_stats(D, ps_yt)
                x1_half(A, 1)
                if D:
                    dve.wait_ge(stats_ready, upto(D[0], TB))
                row_sums(B)
                if D:
                    y_mean_var(D)
                row_sums_inverse(B)
                if D:
                    y_var_eps(D)
                row_denominators(B)
                normalise(B)
                if D:
                    y_shift(D)
                score_bias(A)
                y_half(C, 0)
                keep_scale(C)
                score_sums(A)
                y_half(C, 1)

            def step_from_next_x1(q, r):
                A, B, C, D, N = in_step(q, r)
                if N:
                    x1_half(N, 0)
                x2_half(B, 0)
                block_maxima(A)
                x2_half(B, 1)
                other_maxima(A)
                row_maxima(A)

            step_until_y(0, LOOP_FROM - 1)
            with dve.Fori(0, (LOOP_TO - LOOP_FROM) // 2) as q:
                for r in (LOOP_FROM, LOOP_FROM + 1):
                    step_from_next_x1(q, r - 1)
                    step_until_y(q, r)
            step_from_next_x1(0, LOOP_TO - 1)
            step_until_y(0, LOOP_TO)
            step_from_next_x1(0, LOOP_TO)
            t5, t6, t7 = TAIL
            b, p, n = t7
            dve.wait_ge(out_ready, upto(t6[0] - 2, CH))
            x3_half(t6, 0)
            row_sums(t7)
            x3_half(t6, 1)
            row_sums_inverse(t7)
            y_stats(t5, ps_yt)
            row_denominators(t7)
            normalise(t7)
            dve.wait_ge(stats_ready, upto(t5[0], TB))
            y_mean_var(t5)
            y_var_eps(t5)
            y_shift(t5)
            x2_half(t7, 0)
            x2_half(t7, 1)
            y_half(t6, 0)
            y_half(t6, 1)
            keep_scale(t6)
            x3_half(t7, 0, ps_l2_last)
            x3_half(t7, 1, ps_l2_last)
            y_stats(t6, ps_yt)
            dve.wait_ge(stats_ready, upto(t6[0], TB))
            y_mean_var(t6)
            y_var_eps(t6)
            y_half(t7, 0)
            y_half(t7, 1)
            y_shift(t6)
            keep_scale(t7)
            y_stats(t7, ps_yt_last)
            dve.wait_ge(stats_ready, upto(b, TB))
            y_mean_var(t7)
            y_var_eps(t7)
            for s in range(TB):
                nc.vector.tensor_scalar(centred[:, s, :], ps_yt_last[s], meanvar[p][:, s, 0:1], None, ALU.subtract).then_inc(centred_ready, 1)
            dve.wait_ge(rstd_ready, upto(b))
            dve.wait_ge(centred_ready, TB)
            nc.vector.tensor_scalar(n_tm[p][:, 1, :], centred[:, 1, :], rstd[p][:, 1:2], None, ALU.mult).then_inc(last_n_ready, 1)
            dve.wait_ge(x3b_ready, CH)
            dve.wait_ge(stored[p], 16 * n)
            for m in range(CH):
                dve.wait_ge(nt_done, CH * b + m + 1)
                nc.vector.scalar_tensor_tensor(out_fm[p][:, m, :], ps_n_last[m], gb[p][:, m:m + 1], x3b[:, m, :],
                                               ALU.mult, ALU.add).then_inc(last_out_ready, 1)

        @block.scalar
        def _(act):
            def copy_x1(X):
                b, p, n = X
                act.wait_ge(x1t_done, upto(b))
                nc.scalar.copy(x1_tm[p][:, :, :].rearrange("p s d -> p (s d)"), ps_x1[:, :]).then_inc(x1tm_ready, 1)

            def score_tanh(X):
                b, p, n = X
                act.wait_ge(pre_ready, upto(b))
                nc.scalar.activation(att[p][:, :, :], pre[p][:, :, :], ACT.Tanh).then_inc(tanh_ready, 1)

            def softmax_exps(X):
                b, p, n = X
                act.wait_ge(dkey_ready, upto(b))
                nc.scalar.activation(prob_t[p][:, :, P], dkey[p][:, :], ACT.Exp).then_inc(ekey_ready, 1)
                for j in range(TB):
                    act.wait_ge(nmask_ready, TB * b + j + 1)
                    nc.scalar.activation(prob[p][:, j, :], nmasked[p][:, j, :], ACT.Exp, bias=nmax[p][:, j:j + 1], scale=-1.0,
                                         accum_out=psum_row[p][:, j:j + 1]).then_inc(prob_ready, 1)
                act.wait_ge(dother_ready, upto(b))
                nc.scalar.activation(wother[p][:, :], dother[p][:, :], ACT.Exp).then_inc(wother_ready, 1)

            def copy_probs(X):
                b, p, n = X
                act.wait_ge(probt_done, upto(b))
                nc.scalar.copy(prob_t[p][:, :, 0:P], ps_xp[:, 0:SEQ].rearrange("p (b j) -> p b j", b=TB)).then_inc(probt_ready, 1)
                nc.scalar.copy(wother_all[p][:, :], ps_xp[:, SEQ:2 * SEQ]).then_inc(wall_ready, 1)

            def bottleneck_relu(X):
                b, p, n = X
                act.wait_ge(down_done, upto(b))
                c = CH * BOT + DIM
                nc.scalar.activation(z_fm[p][:, :], down, ACT.Relu, bias=w3_sb[p][:, c:c + 1]).then_inc(z_ready, 1)

            def y_normalise(X, blocks):
                b, p, n = X
                act.wait_ge(nmean_ready, upto(b))
                for s, y in enumerate(blocks):
                    a = nc.scalar.activation(n_tm[p][:, s, :], y, ACT.Identity,
                                             scale=rstd[p][:, s:s + 1], bias=nmean[p][:, s:s + 1])
                a.then_inc(ntm_ready, 1)

            def scale_n(X, chunks):
                b, p, n = X
                act.wait_ge(gb_ready, upto(b))
                act.wait_ge(nt_done, upto(b, CH))
                for m in range(CH):
                    nc.scalar.activation(scaled[p][:, m, :], chunks[m], ACT.Identity,
                                         scale=gb[p][:, m:m + 1], bias=gb[p][:, CH + m:CH + m + 1]).then_inc(scaled_ready, 1)

            act.dma_start(x0_fm[0][:, :, :], xT[0, :, :, :]).then_inc(x0_in[0], 16)
            act.dma_start(w1_sb[:, :, :], w1).then_inc(consts_in, 16)
            act.dma_start(b1_sb[:, :], b1.to_broadcast([P, ATT])).then_inc(consts_in, 16)
            act.dma_start(v_sb[:, :], v.to_broadcast([P, ATT])).then_inc(consts_in, 16)
            act.dma_start(ids_sb[:, :], ids).then_inc(ids_in, 16)
            b0, b1_, b2 = HEAD
            copy_x1(b0)
            score_tanh(b0)
            softmax_exps(b0)
            copy_x1(b1_)
            score_tanh(b1_)
            copy_probs(b0)
            softmax_exps(b1_)

            def step(q, r):
                A, B, C, D, N = in_step(q, r)
                bottleneck_relu(C)
                copy_x1(A)
                if D:
                    y_normalise(D, ps_yt)
                score_tanh(A)
                copy_probs(B)
                if D:
                    scale_n(D, ps_n)
                softmax_exps(A)

            run(act, step)
            t5, t6, t7 = TAIL
            bottleneck_relu(t6)
            copy_probs(t7)
            y_normalise(t5, ps_yt)
            scale_n(t5, ps_n_last)
            bottleneck_relu(t7)
            y_normalise(t6, ps_yt)
            b, p, n = t7
            act.wait_ge(gb_ready, upto(b))
            for m in range(CH):
                nc.scalar.activation(x3b[:, m, :], x3_of(t7)[:, m, :], ACT.Identity, bias=gb[p][:, CH + m:CH + m + 1]).then_inc(x3b_ready, 1)
            scale_n(t6, ps_n_last)
            act.wait_ge(rstd_ready, upto(b))
            act.wait_ge(centred_ready, 1)
            nc.scalar.activation(n_tm[p][:, 0, :], centred[:, 0, :], ACT.Identity, scale=rstd[p][:, 0:1]).then_inc(ntm_ready, 1)

        @block.gpsimd
        def _(pool):
            own = 0

            def made(ins):
                nonlocal own
                own += 1
                ins.then_inc(gp_own, 1)
                pool.wait_ge(gp_own, own)

            made(nc.gpsimd.memset(ones[:, :], 1.0))
            nc.gpsimd.affine_select(out=ident[:, :], in_=ones[:, :], pattern=[[-1, P]], compare_op=ALU.is_equal,
                                    fill=0.0, base=0, channel_multiplier=1).then_inc(ident_ready, 1)
            made(nc.gpsimd.memset(masks[:, :, :], 0.0))
            nc.gpsimd.memset(half_neg[:, :], -0.5)
            part = [masks[:, k, 0:P] for k in range(NTYPES)]
            nc.gpsimd.affine_select(out=part[0], in_=part[0], pattern=[[-1, P]], compare_op=ALU.is_ge,
                                    fill=MASKED, base=0, channel_multiplier=1)
            nc.gpsimd.affine_select(out=part[1], in_=part[1], pattern=[[1, P]], compare_op=ALU.is_ge,
                                    fill=MASKED, base=0, channel_multiplier=-1)
            nc.gpsimd.affine_select(out=part[2], in_=part[2], pattern=[[1, P]], compare_op=ALU.not_equal,
                                    fill=MASKED, base=0, channel_multiplier=-1)
            nc.gpsimd.memset(masks[:, 0, P:P + 1], MASKED)
            nc.gpsimd.memset(masks[:, 1, P + 1:P + 2], MASKED)
            for j in range(TB):
                c = P + TB + j
                nc.gpsimd.iota(masks[:, 0, c:c + 1], pattern=[[1, 1]], base=j * P + 1, channel_multiplier=1,
                               allow_small_or_imprecise_dtypes=True)
                nc.gpsimd.iota(masks[:, 1, c:c + 1], pattern=[[1, 1]], base=SEQ - j * P, channel_multiplier=-1,
                               allow_small_or_imprecise_dtypes=True)
                last = nc.gpsimd.memset(masks[:, 2, c:c + 1], float(SEQ - 1))
            made(last)
            pool.wait_ge(ids_in, 16)

            def choose_mask(X, early=False):
                b, p, n = X
                if not early:
                    pool.wait_ge(nmask_ready, upto(b - 2, TB))
                kind = pool.value_load(ids_sb[0:1, bass.ds(b + BATCHES, 1)], min_val=0, max_val=NTYPES - 1)
                nc.gpsimd.tensor_copy(mask_b[p][:, :], masks[:, bass.ds(kind, 1), :].rearrange("p o n -> p (o n)")).then_inc(mask_ready, 1)

            def y_rstd(X):
                b, p, n = X
                pool.wait_ge(veps_ready, upto(b))
                nc.gpsimd.tensor_tensor(rstd[p][:, :], veps[p][:, :], half_neg[:, :], ALU.pow).then_inc(rstd_ready, 1)

            def output(X):
                b, p, n = X
                if not isinstance(b, int) or b >= 2:
                    pool.wait_ge(stored[p], n * 16)
                for m in range(CH):
                    pool.wait_ge(scaled_ready, CH * b + m + 1)
                    nc.gpsimd.tensor_tensor(out_fm[p][:, m, :], scaled[p][:, m, :], x3_of(X)[:, m, :], ALU.add).then_inc(out_ready, 1)

            b0, b1_, b2 = HEAD
            choose_mask(b0, early=True)
            choose_mask(b1_, early=True)
            choose_mask(b2)

            def step(q, r):
                A, B, C, D, N = in_step(q, r)
                if D:
                    y_rstd(D)
                    output(D)
                if N:
                    choose_mask(N)

            run(pool, step)
            t5, t6, t7 = TAIL
            y_rstd(t5)
            output(t5)
            y_rstd(t6)
            y_rstd(t7)
            output(t6)


def kernel(x, itok_B_0_63, itok_B_0_2, itok_B_0_7, itok_B_0_6, L0_cond_W, L0_cond_b, L1_cond_W1, L1_cond_b1, L1_cond_v,
           L2_cond_weight, L2_cond_bias, L3_cond_down_w, L3_cond_down_b, L3_cond_up_w, L3_cond_up_b, L3_cond_ln_g, L3_cond_ln_b):
    import numpy as np
    import concourse.bacc as bacc
    from concourse.bass_utils import run_bass_kernel_spmd

    def rows(w):
        n, d, m = w.shape
        return w.reshape(n, d // P, P, m).transpose(0, 2, 1, 3).reshape(n, P, -1)

    a = {k: np.asarray(v) for k, v in dict(
        x=x, W0=L0_cond_W, b0=L0_cond_b, W1=L1_cond_W1, b1=L1_cond_b1, v=L1_cond_v, W2=L2_cond_weight, b2=L2_cond_bias,
        Wd=L3_cond_down_w, bd=L3_cond_down_b, Wu=L3_cond_up_w, bu=L3_cond_up_b, g=L3_cond_ln_g, b=L3_cond_ln_b).items()}
    host = {
        "xT": rows(a["x"].transpose(0, 2, 1)).reshape(BATCHES, P, CH, SEQ),
        "w0": np.concatenate([rows(a["W0"]), rows(a["b0"][:, :, None])], axis=2),
        "w1": rows(a["W1"][None]).reshape(P, CH, ATT),
        "b1": a["b1"].reshape(1, ATT),
        "v": a["v"].reshape(1, ATT),
        "w2": np.concatenate([rows(a["W2"].transpose(0, 2, 1)), rows(a["b2"][:, :, None])], axis=2),
        "w3": np.concatenate([rows(a["Wd"]), a["Wu"], a["bd"][:, :, None]]
                             + [rows(a[k][:, :, None]) for k in ("bu", "g", "b")], axis=2),
        "ids": np.concatenate([np.asarray(i) for i in (itok_B_0_63, itok_B_0_2, itok_B_0_7, itok_B_0_6)]).reshape(1, 4 * BATCHES),
    }
    nc = bacc.Bacc("TRN2", target_bir_lowering=False, num_devices=1)
    arrays, args = {}, []
    for name, arr in host.items():
        arr = np.ascontiguousarray(arr)
        arrays[f"{name}_dram"] = arr
        args.append(nc.dram_tensor(f"{name}_dram", arr.shape, mybir.dt.from_np(arr.dtype), kind="ExternalInput").ap())
    args.append(nc.dram_tensor("out_dram", (BATCHES, P, CH, SEQ), F32, kind="ExternalOutput").ap())
    build(nc, *args)
    r = run_bass_kernel_spmd(nc, [arrays], core_ids=[0])
    got = r.results[0]["out_dram"]
    return got.transpose(0, 3, 2, 1).reshape(BATCHES, SEQ, DIM)
```

```python
from contextlib import ExitStack

import concourse.bass as bass
from concourse import mybir

F32 = mybir.dt.float32
I32 = mybir.dt.int32
ALU = mybir.AluOpType
ACT = mybir.ActivationFunctionType
AX = mybir.AxisListType

P = 128
BATCHES, SEQ, DIM = 8, 256, 256
CH = DIM // P
TB = SEQ // P
ATT = 64
BOT = 128
NTYPES = 3
ROW = CH * DIM
W0_COLS = ROW + CH
W2_COLS = ROW + CH
W3_COLS = CH * BOT + DIM + 1
BU, G, B_ROW = range(3)
ROWS_COLS = 3 * DIM
MASK_COLS = P + 2 * TB
MASKED = 1e30
EPS = 1e-5
WARMUP = 4
STAGES = 4
LOOP_FROM, LOOP_TO = 3, 7


def build(nc, xT, w0, w1, b1, v, w2, w3, rows, ids, out):
    with ExitStack() as ctx:
        def sb(name, shape, dt=F32):
            return ctx.enter_context(nc.sbuf_tensor(name, shape, dt))

        def pair(name, shape, dt=F32):
            return [sb(f"{name}{i}", shape, dt) for i in range(2)]

        def bank(name):
            return ctx.enter_context(nc.psum_tensor(name, [P, 512], F32))

        def sem(name):
            return ctx.enter_context(nc.semaphore(name))

        ident = sb("ident", [P, P])
        ones = sb("ones", [P, P])
        masks = sb("masks", [P, NTYPES, MASK_COLS])
        half_neg = sb("half_neg", [P, TB])
        w1_sb = sb("w1_sb", [P, CH, ATT])
        table_warm = sb("table_warm", [P, 1])
        b1_sb = sb("b1_sb", [P, ATT])
        v_sb = sb("v_sb", [P, ATT])
        ids_sb = sb("ids_sb", [1, 4 * BATCHES], I32)
        x0_fm = pair("x0_fm", [P, CH, SEQ])
        w0_sb = pair("w0_sb", [P, W0_COLS])
        x0_third = sb("x0_third", [P, CH, SEQ])
        w0_third = sb("w0_third", [P, W0_COLS])
        w2_sb = pair("w2_sb", [P, W2_COLS])
        w3_sb = pair("w3_sb", [P, W3_COLS])
        rows_sb = pair("rows_sb", [P, ROWS_COLS])
        rows_last = sb("rows_last", [P, ROWS_COLS])
        x1_fm = pair("x1_fm", [P, CH, SEQ])
        x1_tm = pair("x1_tm", [P, TB, DIM])
        pre = pair("pre", [P, TB, ATT])
        att = pair("att", [P, TB, ATT])
        attv = pair("attv", [P, TB, ATT])
        nscore = pair("nscore", [P, TB])
        mask_b = pair("mask_b", [P, MASK_COLS])
        rcount = pair("rcount", [P, TB])
        nbmax = pair("nbmax", [P, TB])
        nbmax_o = pair("nbmax_o", [P, TB])
        dkey = pair("dkey", [P, TB])
        nmasked = pair("nmasked", [P, TB, P])
        nmax = pair("nmax", [P, TB])
        dother = pair("dother", [P, TB])
        prob = pair("prob", [P, TB, P])
        psum_row = pair("psum_row", [P, TB])
        wother = pair("wother", [P, TB])
        rowsum = pair("rowsum", [P, TB])
        rsum = pair("rsum", [P, TB])
        rdenom = pair("rdenom", [P, TB])
        wother_n = pair("wother_n", [P, TB])
        prob_n = pair("prob_n", [P, TB, P])
        prob_t = pair("prob_t", [P, TB, P + 4])
        wother_all = pair("wother_all", [P, SEQ])
        x2_fm = pair("x2_fm", [P, CH, SEQ])
        x3_fm = pair("x3_fm", [P, CH, SEQ])
        z_fm = pair("z_fm", [P, SEQ])
        x3_tm = pair("x3_tm", [P, TB, DIM])
        x3bu = pair("x3bu", [P, TB, DIM])
        x3b = pair("x3b", [P, TB, DIM])
        y_tm = pair("y_tm", [P, TB, DIM])
        stats = pair("stats", [P, TB, 6])
        meanvar = pair("meanvar", [P, TB, 2])
        veps = pair("veps", [P, TB])
        rstd = pair("rstd", [P, TB])
        nmean = pair("nmean", [P, TB])
        n_tm = pair("n_tm", [P, TB, DIM])
        scaled = pair("scaled", [P, TB, DIM])
        out_tm = pair("out_tm", [P, TB, DIM])
        centred = sb("centred", [P, TB, DIM])

        ps_l0 = bank("ps_l0")
        ps_x1 = bank("ps_x1")
        ps_xp = bank("ps_xp")
        ps_du = bank("ps_du")
        ps_pl = bank("ps_pl")
        ps_x3 = bank("ps_x3")
        ps_s = bank("ps_s")
        ps_t = bank("ps_t")
        scores = ps_s[:, 0:SEQ]
        key_sums = ps_s[:, SEQ:SEQ + TB]
        down = ps_du[:, SEQ:2 * SEQ]
        ps_up = [ps_du[:, 0:SEQ], ps_x3[:, 0:SEQ]]
        ps_up_last = [ps_du[:, 0:SEQ], ps_l0[:, 0:SEQ]]
        ps_x3b = [ps_s[:, 0:DIM], ps_s[:, DIM:2 * DIM]]
        ps_l2 = [ps_pl[:, 0:SEQ], ps_x1[:, 0:SEQ]]
        ps_l0_halves = [ps_l0[:, 0:SEQ], ps_l0[:, SEQ:2 * SEQ]]
        ps_l0_first = [ps_l0[:, 0:SEQ], ps_du[:, 0:SEQ]]
        ps_l0_second = [ps_pl[:, 0:SEQ], ps_xp[:, 0:SEQ]]
        ps_l0_third = ps_l0_first
        ps_t_first = [ps_t[:, 0:ATT], ps_x3[:, 0:ATT]]
        ps_pool = [x[:, :].rearrange("p (b n) -> p b n", b=TB) for x in (ps_pl, ps_x3)]
        ps_pool_last = [x[:, :].rearrange("p (b n) -> p b n", b=TB) for x in (ps_pl, ps_t)]

        ids_in = sem("ids_in")
        consts_in = sem("consts_in")
        x0_in = [sem(f"x0_in{i}") for i in range(2)]
        w0_in = [sem(f"w0_in{i}") for i in range(2)]
        x0_third_in = sem("x0_third_in")
        w0_third_in = sem("w0_third_in")
        w2_in = [sem(f"w2_in{i}") for i in range(2)]
        rows_in = [sem(f"rows_in{i}") for i in range(2)]
        rows_last_in = sem("rows_last_in")
        w3_in = [sem(f"w3_in{i}") for i in range(2)]
        stored = [sem(f"stored{i}") for i in range(2)]
        gp_own = sem("gp_own")
        ident_ready = sem("ident_ready")
        l0_done = sem("l0_done")
        down_done = sem("down_done")
        probt_done = sem("probt_done")
        up_done = sem("up_done")
        pool_done = sem("pool_done")
        ksum_done = sem("ksum_done")
        x1t_done = sem("x1t_done")
        att_done = sem("att_done")
        l2_done = sem("l2_done")
        x3t_done = sem("x3t_done")
        last_x3b_done = sem("last_x3b_done")
        score_done = sem("score_done")
        nbmax_ready = sem("nbmax_ready")
        nbmax_o_ready = sem("nbmax_o_ready")
        dkey_ready = sem("dkey_ready")
        nmask_ready = sem("nmask_ready")
        dother_ready = sem("dother_ready")
        rowsum_ready = sem("rowsum_ready")
        probn_ready = sem("probn_ready")
        wothern_ready = sem("wothern_ready")
        x1fm_ready = sem("x1fm_ready")
        rcount_ready = sem("rcount_ready")
        rsum_ready = sem("rsum_ready")
        veps_ready = sem("veps_ready")
        rdenom_ready = sem("rdenom_ready")
        x2fm_ready = sem("x2fm_ready")
        pre_ready = sem("pre_ready")
        nscore_ready = sem("nscore_ready")
        y_ready = sem("y_ready")
        x3bu_ready = sem("x3bu_ready")
        stats_ready = sem("stats_ready")
        meanvar_ready = sem("meanvar_ready")
        nmean_ready = sem("nmean_ready")
        x3fm_ready = sem("x3fm_ready")
        x3b_ready = sem("x3b_ready")
        centred_ready = sem("centred_ready")
        last_out_ready = sem("last_out_ready")
        vector_out_ready = sem("vector_out_ready")
        ekey_ready = sem("ekey_ready")
        wother_ready = sem("wother_ready")
        prob_ready = sem("prob_ready")
        z_ready = sem("z_ready")
        x3tm_ready = sem("x3tm_ready")
        probt_ready = sem("probt_ready")
        wall_ready = sem("wall_ready")
        x1tm_ready = sem("x1tm_ready")
        tanh_ready = sem("tanh_ready")
        ntm_ready = sem("ntm_ready")
        first_n_ready = sem("first_n_ready")
        mask_ready = sem("mask_ready")
        rstd_ready = sem("rstd_ready")
        scaled_ready = sem("scaled_ready")
        first_scaled_ready = sem("first_scaled_ready")
        out_ready = sem("out_ready")

        def run(eng, step):
            step(0, LOOP_FROM - 1)
            with eng.Fori(0, (LOOP_TO - LOOP_FROM) // 2) as q:
                step(q, LOOP_FROM)
                step(q, LOOP_FROM + 1)
            step(0, LOOP_TO)

        def batch(q, r):
            if isinstance(q, int) and not 0 <= 2 * q + r < BATCHES:
                return None
            return 2 * q + r, r % 2, q + r // 2

        def upto(b, per_batch=1):
            return b * per_batch + per_batch

        def row_of(buffer, r):
            return buffer[:, r * DIM:(r + 1) * DIM].rearrange("p (o d) -> p o d", o=1).to_broadcast([P, TB, DIM])

        def l0_operands(X):
            b, p, n = X
            if whole_before(X):
                return x0_third, w0_third, x0_third_in, w0_third_in, 16
            earlier = n if p == 1 or (isinstance(b, int) and b == 0) else n - 1
            return x0_fm[p], w0_sb[p], x0_in[p], w0_in[p], (earlier + 1) * 16

        def whole_before(X):
            return isinstance(X[0], int) and X[0] == 2

        def in_step(q, r):
            return [batch(q, r - s) for s in range(STAGES)] + [batch(q, r + 1)]

        HEAD = [batch(0, b) for b in range(3)]
        TAIL = [batch(0, b) for b in range(BATCHES - 3, BATCHES)]

        block = ctx.enter_context(nc.Block())

        @block.sync
        def _(sp):
            def row(table, b, field, n):
                return sp.value_load(table[0:1, bass.ds(b + field * BATCHES, 1)], min_val=0, max_val=n - 1)

            def load_w0(X, early=False):
                b, p, n = X
                i = row(ids if early else ids_sb, b, 0, w0.shape[0])
                x0, w0b, x0_loaded, w0_loaded, count = l0_operands(X)
                if not early:
                    sp.wait_ge(l0_done, upto(b - 2, CH))
                    sp.wait_ge(x1fm_ready, upto(b - 2, CH))
                sp.dma_start(w0b[:, :], w0[bass.ds(i, 1), :, :].rearrange("o p n -> (o p) n")).then_inc(w0_loaded, 16)

            def load_w2(X, early=False):
                b, p, n = X
                i = row(ids if early else ids_sb, b, 2, w2.shape[0])
                if not early:
                    sp.wait_ge(l2_done, upto(b - 2, CH))
                    sp.wait_ge(x3fm_ready, upto(b - 2, CH))
                sp.dma_start(w2_sb[p][:, :], w2[bass.ds(i, 1), :, :].rearrange("o p n -> (o p) n")).then_inc(w2_in[p], 16)

            def load_w3(X, early=False):
                b, p, n = X
                i = row(ids if early else ids_sb, b, 3, w3.shape[0])
                if not early:
                    sp.wait_ge(y_ready, upto(b - 2, TB))
                sp.dma_start(w3_sb[p][:, :], w3[bass.ds(i, 1), :, :].rearrange("o p n -> (o p) n")).then_inc(w3_in[p], 16)

            def load_rows(X, early=False):
                b, p, n = X
                i = row(ids if early else ids_sb, b, 3, w3.shape[0])
                if not early:
                    sp.wait_ge(scaled_ready, upto(b - 2))
                sp.dma_start(rows_sb[p][:, :], rows[bass.ds(i, 1), :].to_broadcast([P, ROWS_COLS])).then_inc(rows_in[p], 16)

            def store(X):
                b, p, n = X
                sp.wait_ge(out_ready, upto(b))
                sp.dma_start(out[bass.ds(b, 1), :, :, :].rearrange("o p s d -> (o p) s d"), out_tm[p][:, :, :]).then_inc(stored[p], 16)

            b0, b1_, b2 = HEAD
            load_w0(b0, early=True)
            load_w0(b1_, early=True)
            load_w2(b0, early=True)
            sp.wait_ge(ids_in, 16)
            load_w0(b2, early=True)
            load_w2(b1_, early=True)
            load_w3(b0, early=True)
            load_rows(b0, early=True)

            def step(q, r):
                A, B, C, D, N = in_step(q, r)
                if N:
                    load_w0(N)
                load_w2(A)
                load_w3(B, early=isinstance(q, int) and B[0] < 2)
                load_rows(B, early=isinstance(q, int) and B[0] < 2)
                if D:
                    store(D)

            run(sp, step)
            t5, t6, t7 = TAIL
            load_w3(t7)
            i = row(ids_sb, t7[0], 3, w3.shape[0])
            sp.dma_start(rows_last[:, :], rows[bass.ds(i, 1), :].to_broadcast([P, ROWS_COLS])).then_inc(rows_last_in, 16)
            store(t5)
            def store_block(X, s, ready, count):
                b, p, n = X
                sp.wait_ge(ready, count)
                sp.dma_start(out[b, :, s, :], out_tm[p][:, s, :]).then_inc(stored[p], 16)

            store_block(t6, 0, out_ready, upto(t6[0]))
            store_block(t7, 0, last_out_ready, 1)
            store_block(t7, 1, last_out_ready, 2)
            store_block(t6, 1, vector_out_ready, 1)
            for parity_stored in stored:
                sp.wait_ge(parity_stored, 16 * (BATCHES // 2 - 1 + TB))

        @block.tensor
        def _(pe):
            def l0_half(X, m, banks=ps_l0_halves):
                b, p, n = X
                x0, w0b, x0_loaded, w0_loaded, count = l0_operands(X)
                if m == 0:
                    pe.wait_ge(x0_loaded, count)
                    pe.wait_ge(w0_loaded, count)
                elif banks is ps_l0_halves:
                    pe.wait_ge(x1fm_ready, CH * b + 1)
                for k in range(CH):
                    mm = nc.tensor.matmul(banks[m], w0b[:, k * DIM + m * P:k * DIM + (m + 1) * P],
                                          x0[:, k, :], start=(k == 0), stop=(k == CH - 1))
                mm.then_inc(l0_done, 1)

            def x1_to_tm(X):
                b, p, n = X
                pe.wait_ge(x1fm_ready, upto(b, CH))
                for k in range(CH):
                    for s in range(TB):
                        mm = nc.tensor.transpose(ps_x1[:, s * DIM + k * P:s * DIM + (k + 1) * P],
                                                 x1_fm[p][:, k, s * P:(s + 1) * P], ident[:, :])
                mm.then_inc(x1t_done, 1)

            def score_layer(X):
                b, p, n = X
                for s in range(TB):
                    for k in range(CH):
                        mm = nc.tensor.matmul(ps_t[:, s * ATT:(s + 1) * ATT], x1_fm[p][:, k, s * P:(s + 1) * P],
                                              w1_sb[:, k, :], start=(k == 0), stop=(k == CH - 1))
                mm.then_inc(att_done, 1)

            def score_rows(X):
                b, p, n = X
                pe.wait_ge(nscore_ready, upto(b, TB))
                for l in range(TB):
                    mm = nc.tensor.transpose(scores[:, l * P:(l + 1) * P], nscore[p][:, l:l + 1].to_broadcast([P, P]), ident[:, :])
                mm.then_inc(score_done, 1)

            def key_sum_rows(X):
                b, p, n = X
                pe.wait_ge(ekey_ready, upto(b))
                pe.wait_ge(nmask_ready, upto(b, TB))
                nc.tensor.matmul(key_sums, ones[:, :], prob_t[p][:, :, P], start=True, stop=True).then_inc(ksum_done, 1)

            def transpose_probs(X):
                b, p, n = X
                pe.wait_ge(wothern_ready, upto(b))
                for j in range(TB):
                    nc.tensor.transpose(ps_xp[:, SEQ + j * P:SEQ + (j + 1) * P], wother_n[p][:, j:j + 1].to_broadcast([P, P]), ident[:, :])
                pe.wait_ge(probn_ready, upto(b, TB))
                for j in range(TB):
                    mm = nc.tensor.transpose(ps_xp[:, j * P:(j + 1) * P], prob_n[p][:, j, :], ident[:, :])
                mm.then_inc(probt_done, 1)

            def pool_half(X, m, banks=ps_pool):
                b, p, n = X
                pe.wait_ge(probt_ready, upto(b))
                for j in range(TB):
                    mm = nc.tensor.matmul(banks[m][:, j, 0:P + 1], x1_tm[p][:, j, m * P:(m + 1) * P],
                                          prob_t[p][:, j, 0:P + 1], start=True, stop=True)
                mm.then_inc(pool_done, 1)

            def l2(X, banks):
                b, p, n = X
                pe.wait_ge(w2_in[p], (n + 1) * 16)
                for k in range(CH):
                    pe.wait_ge(x2fm_ready, TB * CH * b + TB * (k + 1))
                    for m in range(CH):
                        mm = nc.tensor.matmul(banks[m], w2_sb[p][:, k * DIM + m * P:k * DIM + (m + 1) * P],
                                              x2_fm[p][:, k, :], start=(k == 0), stop=(k == CH - 1))
                        if k == CH - 1:
                            mm.then_inc(l2_done, 1)

            def adapter_down(X):
                b, p, n = X
                pe.wait_ge(w3_in[p], (n + 1) * 16)
                for k in range(CH):
                    pe.wait_ge(x3fm_ready, CH * b + k + 1)
                    mm = nc.tensor.matmul(down, w3_sb[p][:, k * BOT:(k + 1) * BOT], x3_fm[p][:, k, :],
                                          start=(k == 0), stop=(k == CH - 1))
                mm.then_inc(down_done, 1)

            def x3_to_tm(X):
                b, p, n = X
                for k in range(CH):
                    pe.wait_ge(x3fm_ready, CH * b + k + 1)
                    for s in range(TB):
                        mm = nc.tensor.transpose(ps_x3[:, s * DIM + k * P:s * DIM + (k + 1) * P],
                                                 x3_fm[p][:, k, s * P:(s + 1) * P], ident[:, :])
                mm.then_inc(x3t_done, 1)

            def adapter_up(X, banks=ps_up):
                b, p, n = X
                pe.wait_ge(z_ready, upto(b))
                for s in range(TB):
                    if s == 1 and banks is ps_up:
                        pe.wait_ge(x3tm_ready, upto(b))
                    nc.tensor.matmul(banks[s], z_fm[p][:, s * P:(s + 1) * P], w3_sb[p][:, CH * BOT:CH * BOT + DIM],
                                     start=True, stop=True).then_inc(up_done, 1)

            pe.wait_ge(ident_ready, 1)
            for _ in range(WARMUP):
                nc.tensor.matmul(ps_x3[:, 0:2 * P], ident[:, :], ident[:, :].rearrange("p (o n) -> p o n", o=1).to_broadcast([P, 2, P]),
                                 start=True, stop=True)
            b0, b1_, b2 = HEAD
            l0_half(b0, 0, ps_l0_first)
            l0_half(b0, 1, ps_l0_first)
            pe.wait_ge(consts_in, 48)
            for k in range(CH):
                pe.wait_ge(x1fm_ready, k + 1)
                for s in range(TB):
                    mm = nc.tensor.matmul(ps_t_first[s], x1_fm[0][:, k, s * P:(s + 1) * P], w1_sb[:, k, :],
                                          start=(k == 0), stop=(k == CH - 1))
            mm.then_inc(att_done, 1)
            x1_to_tm(b0)
            l0_half(b1_, 0, ps_l0_second)
            score_rows(b0)
            l0_half(b1_, 1, ps_l0_second)
            l0_half(b2, 0, ps_l0_third)
            key_sum_rows(b0)
            x1_to_tm(b1_)
            score_layer(b1_)
            transpose_probs(b0)
            l0_half(b2, 1, ps_l0_third)
            pool_half(b0, 0)
            pool_half(b0, 1)
            score_rows(b1_)
            pe.wait_ge(x1tm_ready, upto(1))
            l2(b0, ps_l2)

            def step(q, r):
                A, B, C, D, N = in_step(q, r)
                if not whole_before(A):
                    l0_half(A, 1)
                key_sum_rows(B)
                adapter_down(C)
                x3_to_tm(C)
                x1_to_tm(A)
                adapter_up(C)
                transpose_probs(B)
                score_layer(A)
                pool_half(B, 0)
                pe.wait_ge(y_ready, upto(C[0], TB))
                pool_half(B, 1)
                if N:
                    l0_half(N, 0)
                score_rows(A)
                pe.wait_ge(x1tm_ready, upto(A[0]))
                l2(B, ps_l2)

            run(pe, step)
            t5, t6, t7 = TAIL
            key_sum_rows(t7)
            adapter_down(t6)
            transpose_probs(t7)
            x3_to_tm(t6)
            pool_half(t7, 0, ps_pool_last)
            pool_half(t7, 1, ps_pool_last)
            adapter_up(t6)
            l2(t7, ps_l2)
            adapter_down(t7)
            pe.wait_ge(y_ready, upto(t6[0], TB))
            x3_to_tm(t7)
            adapter_up(t7, ps_up_last)
            b, p, n = t7
            pe.wait_ge(rows_last_in, 16)
            for s in range(TB):
                nc.tensor.matmul(ps_x3b[s], ones[0:1, :], rows_last[0:1, B_ROW * DIM:(B_ROW + 1) * DIM], start=True, stop=False)
                for k in range(CH):
                    mm = nc.tensor.matmul(ps_x3b[s][:, k * P:(k + 1) * P], x3_fm[p][:, k, s * P:(s + 1) * P], ident[:, :],
                                          start=False, stop=(k == CH - 1))
            mm.then_inc(last_x3b_done, 1)

        @block.vector
        def _(dve):
            def x1_half(X, m, banks=ps_l0_halves):
                b, p, n = X
                x0, w0b, x0_loaded, w0_loaded, count = l0_operands(X)
                dve.wait_ge(l0_done, CH * b + m + 1)
                nc.vector.scalar_tensor_tensor(x1_fm[p][:, m, :], banks[m], w0b[:, ROW + m:ROW + m + 1],
                                               x0[:, m, :], ALU.add, ALU.add).then_inc(x1fm_ready, 1)

            def score_bias(X):
                b, p, n = X
                dve.wait_ge(att_done, upto(b))
                nc.vector.tensor_tensor(pre[p][:, :, :], ps_t[:, 0:TB * ATT].rearrange("p (s a) -> p s a", s=TB),
                                        b1_sb[:, :].rearrange("p (o a) -> p o a", o=1).to_broadcast([P, TB, ATT]), ALU.add).then_inc(pre_ready, 1)

            def score_sums(X):
                b, p, n = X
                dve.wait_ge(consts_in, 48)
                dve.wait_ge(tanh_ready, upto(b))
                for s in range(TB):
                    nc.vector.tensor_tensor_reduce(attv[p][:, s, :], att[p][:, s, :], v_sb[:, :], -1.0, 0.0,
                                                   ALU.mult, ALU.add, nscore[p][:, s:s + 1]).then_inc(nscore_ready, 1)

            def block_maxima(X):
                b, p, n = X
                dve.wait_ge(mask_ready, upto(b))
                dve.wait_ge(score_done, upto(b))
                nc.vector.reciprocal(rcount[p][:, :], mask_b[p][:, P + TB:P + 2 * TB]).then_inc(rcount_ready, 1)
                nc.vector.tensor_reduce(nbmax[p][:, :], scores.rearrange("p (b l) -> p b l", b=TB), AX.X, ALU.min).then_inc(nbmax_ready, 1)

            def other_maxima(X):
                b, p, n = X
                dve.wait_ge(nbmax_ready, upto(b))
                for j in range(TB):
                    nc.vector.tensor_tensor(nbmax_o[p][:, j:j + 1], nbmax[p][:, 1 - j:2 - j], mask_b[p][:, P + j:P + j + 1], ALU.add).then_inc(nbmax_o_ready, 1)
                dve.wait_ge(nbmax_o_ready, upto(b, TB))
                nc.vector.tensor_tensor(dkey[p][:, :], nbmax[p][:, :], nscore[p][:, :], ALU.subtract).then_inc(dkey_ready, 1)

            def row_maxima(X):
                b, p, n = X
                for j in range(TB):
                    nc.vector.tensor_tensor_reduce(nmasked[p][:, j, :], scores[:, j * P:(j + 1) * P], mask_b[p][:, 0:P],
                                                   1.0, nbmax_o[p][:, j:j + 1], ALU.add, ALU.min, nmax[p][:, j:j + 1]).then_inc(nmask_ready, 1)
                dve.wait_ge(nmask_ready, upto(b, TB))
                nc.vector.tensor_tensor(dother[p][:, :], nmax[p][:, :], nbmax_o[p][:, :], ALU.subtract).then_inc(dother_ready, 1)

            def row_sums(X):
                b, p, n = X
                dve.wait_ge(prob_ready, upto(b, TB))
                dve.wait_ge(wother_ready, upto(b))
                dve.wait_ge(ksum_done, upto(b))
                for j in range(TB):
                    nc.vector.scalar_tensor_tensor(rowsum[p][:, j:j + 1], wother[p][:, j:j + 1], key_sums[:, 1 - j:2 - j],
                                                   psum_row[p][:, j:j + 1], ALU.mult, ALU.add).then_inc(rowsum_ready, 1)

            def row_sums_inverse(X):
                b, p, n = X
                dve.wait_ge(rowsum_ready, upto(b, TB))
                nc.vector.reciprocal(rsum[p][:, :], rowsum[p][:, :]).then_inc(rsum_ready, 1)

            def row_denominators(X):
                b, p, n = X
                dve.wait_ge(rsum_ready, upto(b))
                dve.wait_ge(rcount_ready, upto(b))
                nc.vector.tensor_tensor(rdenom[p][:, :], rsum[p][:, :], rcount[p][:, :], ALU.mult).then_inc(rdenom_ready, 1)

            def normalise(X):
                b, p, n = X
                dve.wait_ge(rdenom_ready, upto(b))
                nc.vector.tensor_tensor(wother_n[p][:, :], wother[p][:, :], rdenom[p][:, :], ALU.mult).then_inc(wothern_ready, 1)
                for j in range(TB):
                    nc.vector.scalar_tensor_tensor(prob_n[p][:, j, :], prob[p][:, j, :], rdenom[p][:, j:j + 1], ident[:, :],
                                                   ALU.mult, ALU.add).then_inc(probn_ready, 1)

            def x2_half(X, m, banks=ps_pool):
                b, p, n = X
                if m == 0:
                    dve.wait_ge(wall_ready, upto(b))
                dve.wait_ge(pool_done, CH * b + m + 1)
                for j in range(TB):
                    nc.vector.scalar_tensor_tensor(x2_fm[p][:, m, j * P:(j + 1) * P], wother_all[p][:, j * P:(j + 1) * P],
                                                   banks[m][:, 1 - j, P:P + 1], banks[m][:, j, 0:P],
                                                   ALU.mult, ALU.add).then_inc(x2fm_ready, 1)

            def x3_half(X, m, banks=ps_l2):
                b, p, n = X
                dve.wait_ge(l2_done, CH * b + m + 1)
                nc.vector.scalar_tensor_tensor(x3_fm[p][:, m, :], banks[m], w2_sb[p][:, ROW + m:ROW + m + 1],
                                               x2_fm[p][:, m, :], ALU.add, ALU.add).then_inc(x3fm_ready, 1)

            def up_residual(X):
                b, p, n = X
                dve.wait_ge(rows_in[p], (n + 1) * 16)
                dve.wait_ge(x3tm_ready, upto(b))
                nc.vector.tensor_tensor(x3bu[p][:, :, :], x3_tm[p][:, :, :], row_of(rows_sb[p], BU), ALU.add).then_inc(x3bu_ready, 1)

            def y_block(X, s, banks=ps_up):
                b, p, n = X
                if s == 0:
                    dve.wait_ge(x3bu_ready, upto(b))
                dve.wait_ge(up_done, TB * b + s + 1)
                nc.vector.tensor_tensor(y_tm[p][:, s, :], banks[s], x3bu[p][:, s, :], ALU.add).then_inc(y_ready, 1)

            def y_stats(X, s):
                b, p, n = X
                dve.wait_ge(y_ready, TB * b + s + 1)
                nc.vector.bn_stats(stats[p][:, s, :], y_tm[p][:, s, :]).then_inc(stats_ready, 1)

            def y_mean_var(X):
                b, p, n = X
                for s in range(TB):
                    nc.vector.bn_aggr(meanvar[p][:, s, :], stats[p][:, s, :]).then_inc(meanvar_ready, 1)

            def y_var_eps(X):
                b, p, n = X
                dve.wait_ge(meanvar_ready, upto(b, TB))
                nc.vector.tensor_scalar(veps[p][:, :], meanvar[p][:, :, 1], EPS, None, ALU.add).then_inc(veps_ready, 1)

            def y_shift(X):
                b, p, n = X
                dve.wait_ge(rstd_ready, upto(b))
                nc.vector.scalar_tensor_tensor(nmean[p][:, :], meanvar[p][:, :, 0], -1.0, rstd[p][:, :], ALU.mult, ALU.mult).then_inc(nmean_ready, 1)

            dve.wait_ge(consts_in, 48)
            dve.wait_ge(ident_ready, 1)
            b0, b1_, b2 = HEAD
            x1_half(b0, 0, ps_l0_first)
            x1_half(b0, 1, ps_l0_first)
            dve.wait_ge(att_done, 1)
            nc.vector.tensor_tensor(pre[0][:, 0, :], ps_t_first[0], b1_sb[:, :], ALU.add)
            nc.vector.tensor_tensor(pre[0][:, 1, :], ps_t_first[1], b1_sb[:, :], ALU.add).then_inc(pre_ready, 1)
            score_sums(b0)
            x1_half(b1_, 0, ps_l0_second)
            block_maxima(b0)
            other_maxima(b0)
            row_maxima(b0)
            x1_half(b1_, 1, ps_l0_second)
            row_sums(b0)
            row_sums_inverse(b0)
            row_denominators(b0)
            normalise(b0)
            score_bias(b1_)
            score_sums(b1_)
            x1_half(b2, 0, ps_l0_third)
            x1_half(b2, 1, ps_l0_third)
            x2_half(b0, 0)
            x2_half(b0, 1)
            block_maxima(b1_)
            other_maxima(b1_)
            row_maxima(b1_)

            def step_until_pooling(q, r):
                A, B, C, D, N = in_step(q, r)
                x3_half(C, 0)
                x3_half(C, 1)
                if not whole_before(A):
                    x1_half(A, 1)
                if D:
                    dve.wait_ge(stats_ready, upto(D[0], TB))
                row_sums(B)
                if D:
                    y_mean_var(D)
                row_sums_inverse(B)
                if D:
                    y_var_eps(D)
                row_denominators(B)
                normalise(B)
                if D:
                    y_shift(D)
                up_residual(C)
                y_block(C, 0)
                y_block(C, 1)
                y_stats(C, 0)
                y_stats(C, 1)
                score_bias(A)

            def step_from_pooling(q, r):
                A, B, C, D, N = in_step(q, r)
                x2_half(B, 0)
                score_sums(A)
                x2_half(B, 1)
                if N:
                    x1_half(N, 0)
                block_maxima(A)
                other_maxima(A)
                row_maxima(A)

            step_until_pooling(0, LOOP_FROM - 1)
            with dve.Fori(0, (LOOP_TO - LOOP_FROM) // 2) as q:
                for r in (LOOP_FROM, LOOP_FROM + 1):
                    step_from_pooling(q, r - 1)
                    step_until_pooling(q, r)
            step_from_pooling(0, LOOP_TO - 1)
            step_until_pooling(0, LOOP_TO)
            step_from_pooling(0, LOOP_TO)
            t5, t6, t7 = TAIL
            x3_half(t6, 0)
            row_sums(t7)
            x3_half(t6, 1)
            row_sums_inverse(t7)
            row_denominators(t7)
            normalise(t7)
            dve.wait_ge(stats_ready, upto(t5[0], TB))
            y_mean_var(t5)
            y_var_eps(t5)
            y_shift(t5)
            x2_half(t7, 0, ps_pool_last)
            x2_half(t7, 1, ps_pool_last)
            up_residual(t6)
            y_block(t6, 0)
            y_block(t6, 1)
            x3_half(t7, 0)
            x3_half(t7, 1)
            y_stats(t6, 0)
            y_stats(t6, 1)
            dve.wait_ge(stats_ready, upto(t6[0], TB))
            y_mean_var(t6)
            y_var_eps(t6)
            b, p, n = t7
            dve.wait_ge(rows_last_in, 16)
            dve.wait_ge(x3t_done, upto(b))
            nc.vector.tensor_tensor(x3bu[p][:, :, :], ps_x3[:, :].rearrange("p (s d) -> p s d", s=TB), row_of(rows_last, BU),
                                    ALU.add).then_inc(x3bu_ready, 1)
            y_shift(t6)
            y_block(t7, 0, ps_up_last)
            y_block(t7, 1, ps_up_last)
            y_stats(t7, 0)
            y_stats(t7, 1)
            dve.wait_ge(stats_ready, upto(b, TB))
            y_mean_var(t7)
            y_var_eps(t7)
            for s in range(TB):
                nc.vector.scalar_tensor_tensor(centred[:, s, :], y_tm[p][:, s, :], meanvar[p][:, s, 0:1],
                                               rows_last[:, G * DIM:(G + 1) * DIM], ALU.subtract, ALU.mult).then_inc(centred_ready, 1)
            dve.wait_ge(centred_ready, TB)
            dve.wait_ge(last_x3b_done, 1)
            dve.wait_ge(stored[p], 16 * n)
            dve.wait_ge(rstd_ready, upto(b))
            for s in range(TB):
                nc.vector.scalar_tensor_tensor(out_tm[p][:, s, :], centred[:, s, :], rstd[p][:, s:s + 1], ps_x3b[s],
                                               ALU.mult, ALU.add).then_inc(last_out_ready, 1)
            b, p, n = t6
            dve.wait_ge(scaled_ready, upto(b))
            dve.wait_ge(x3b_ready, upto(b))
            dve.wait_ge(stored[p], 16 * n)
            nc.vector.tensor_tensor(out_tm[p][:, 1, :], scaled[p][:, 1, :], x3b[p][:, 1, :], ALU.add).then_inc(vector_out_ready, 1)

        @block.scalar
        def _(act):
            def load_x(X, early=False):
                b, p, n = X
                if not early:
                    act.wait_ge(l0_done, upto(b - 2, CH))
                    act.wait_ge(x1fm_ready, upto(b - 2, CH))
                x0, w0b, x0_loaded, w0_loaded, count = l0_operands(X)
                act.dma_start(x0[:, :, :], xT[bass.ds(b, 1), :, :, :].rearrange("o p c s -> (o p) c s")).then_inc(x0_loaded, 16)

            def copy_x1(X):
                b, p, n = X
                act.wait_ge(x1t_done, upto(b))
                nc.scalar.copy(x1_tm[p][:, :, :].rearrange("p s d -> p (s d)"), ps_x1[:, :]).then_inc(x1tm_ready, 1)

            def score_tanh(X):
                b, p, n = X
                act.wait_ge(pre_ready, upto(b))
                nc.scalar.activation(att[p][:, :, :], pre[p][:, :, :], ACT.Tanh).then_inc(tanh_ready, 1)

            def softmax_exps(X):
                b, p, n = X
                act.wait_ge(dkey_ready, upto(b))
                nc.scalar.activation(prob_t[p][:, :, P], dkey[p][:, :], ACT.Exp).then_inc(ekey_ready, 1)
                for j in range(TB):
                    act.wait_ge(nmask_ready, TB * b + j + 1)
                    nc.scalar.activation(prob[p][:, j, :], nmasked[p][:, j, :], ACT.Exp, bias=nmax[p][:, j:j + 1], scale=-1.0,
                                         accum_out=psum_row[p][:, j:j + 1]).then_inc(prob_ready, 1)
                act.wait_ge(dother_ready, upto(b))
                nc.scalar.activation(wother[p][:, :], dother[p][:, :], ACT.Exp).then_inc(wother_ready, 1)

            def copy_probs(X):
                b, p, n = X
                act.wait_ge(probt_done, upto(b))
                nc.scalar.copy(prob_t[p][:, :, 0:P], ps_xp[:, 0:SEQ].rearrange("p (b j) -> p b j", b=TB)).then_inc(probt_ready, 1)
                nc.scalar.copy(wother_all[p][:, :], ps_xp[:, SEQ:2 * SEQ]).then_inc(wall_ready, 1)

            def bottleneck_relu(X):
                b, p, n = X
                act.wait_ge(down_done, upto(b))
                c = CH * BOT + DIM
                nc.scalar.activation(z_fm[p][:, :], down, ACT.Relu, bias=w3_sb[p][:, c:c + 1]).then_inc(z_ready, 1)

            def copy_x3(X):
                b, p, n = X
                act.wait_ge(x3t_done, upto(b))
                nc.scalar.copy(x3_tm[p][:, :, :].rearrange("p s d -> p (s d)"), ps_x3[:, :]).then_inc(x3tm_ready, 1)

            def y_normalise(X):
                b, p, n = X
                act.wait_ge(nmean_ready, upto(b))
                for s in range(TB):
                    a = nc.scalar.activation(n_tm[p][:, s, :], y_tm[p][:, s, :], ACT.Identity,
                                             scale=rstd[p][:, s:s + 1], bias=nmean[p][:, s:s + 1])
                a.then_inc(ntm_ready, 1)

            b0, b1_, b2 = HEAD
            load_x(b0, early=True)
            act.dma_start(w1_sb[:, :, :], w1).then_inc(consts_in, 16)
            act.dma_start(b1_sb[:, :], b1.to_broadcast([P, ATT])).then_inc(consts_in, 16)
            act.dma_start(v_sb[:, :], v.to_broadcast([P, ATT])).then_inc(consts_in, 16)
            act.dma_start(ids_sb[:, :], ids).then_inc(ids_in, 16)
            load_x(b1_, early=True)
            act.wait_ge(ident_ready, 1)
            nc.scalar.activation(table_warm[:, :], ones[:, 0:1], ACT.Exp)
            load_x(b2, early=True)
            score_tanh(b0)
            copy_x1(b0)
            softmax_exps(b0)
            copy_x1(b1_)
            score_tanh(b1_)
            copy_probs(b0)
            softmax_exps(b1_)

            def step(q, r):
                A, B, C, D, N = in_step(q, r)
                if N:
                    load_x(N)
                bottleneck_relu(C)
                copy_x3(C)
                copy_x1(A)
                copy_probs(B)
                score_tanh(A)
                if D:
                    y_normalise(D)
                softmax_exps(A)

            run(act, step)
            t5, t6, t7 = TAIL
            bottleneck_relu(t6)
            copy_probs(t7)
            copy_x3(t6)
            y_normalise(t5)
            bottleneck_relu(t7)
            b, p, n = t6
            act.wait_ge(nmean_ready, upto(b))
            for s, ready in enumerate((first_n_ready, ntm_ready)):
                nc.scalar.activation(n_tm[p][:, s, :], y_tm[p][:, s, :], ACT.Identity,
                                     scale=rstd[p][:, s:s + 1], bias=nmean[p][:, s:s + 1]).then_inc(ready, 1)

        @block.gpsimd
        def _(pool):
            own = 0

            def made(ins):
                nonlocal own
                own += 1
                ins.then_inc(gp_own, 1)
                pool.wait_ge(gp_own, own)

            made(nc.gpsimd.memset(ones[:, :], 1.0))
            nc.gpsimd.affine_select(out=ident[:, :], in_=ones[:, :], pattern=[[-1, P]], compare_op=ALU.is_equal,
                                    fill=0.0, base=0, channel_multiplier=1).then_inc(ident_ready, 1)
            made(nc.gpsimd.memset(masks[:, :, :], 0.0))
            nc.gpsimd.memset(half_neg[:, :], -0.5)
            part = [masks[:, k, 0:P] for k in range(NTYPES)]
            nc.gpsimd.affine_select(out=part[0], in_=part[0], pattern=[[-1, P]], compare_op=ALU.is_ge,
                                    fill=MASKED, base=0, channel_multiplier=1)
            nc.gpsimd.affine_select(out=part[1], in_=part[1], pattern=[[1, P]], compare_op=ALU.is_ge,
                                    fill=MASKED, base=0, channel_multiplier=-1)
            nc.gpsimd.affine_select(out=part[2], in_=part[2], pattern=[[1, P]], compare_op=ALU.not_equal,
                                    fill=MASKED, base=0, channel_multiplier=-1)
            nc.gpsimd.memset(masks[:, 0, P:P + 1], MASKED)
            nc.gpsimd.memset(masks[:, 1, P + 1:P + 2], MASKED)
            for j in range(TB):
                c = P + TB + j
                nc.gpsimd.iota(masks[:, 0, c:c + 1], pattern=[[1, 1]], base=j * P + 1, channel_multiplier=1,
                               allow_small_or_imprecise_dtypes=True)
                nc.gpsimd.iota(masks[:, 1, c:c + 1], pattern=[[1, 1]], base=SEQ - j * P, channel_multiplier=-1,
                               allow_small_or_imprecise_dtypes=True)
                last = nc.gpsimd.memset(masks[:, 2, c:c + 1], float(SEQ - 1))
            made(last)
            pool.wait_ge(ids_in, 16)

            def choose_mask(X, early=False):
                b, p, n = X
                if not early:
                    pool.wait_ge(nmask_ready, upto(b - 2, TB))
                kind = pool.value_load(ids_sb[0:1, bass.ds(b + BATCHES, 1)], min_val=0, max_val=NTYPES - 1)
                nc.gpsimd.tensor_copy(mask_b[p][:, :], masks[:, bass.ds(kind, 1), :].rearrange("p o n -> p (o n)")).then_inc(mask_ready, 1)

            def y_rstd(X):
                b, p, n = X
                pool.wait_ge(veps_ready, upto(b))
                nc.gpsimd.tensor_tensor(rstd[p][:, :], veps[p][:, :], half_neg[:, :], ALU.pow).then_inc(rstd_ready, 1)

            def output_residual(X):
                b, p, n = X
                pool.wait_ge(rows_in[p], (n + 1) * 16)
                pool.wait_ge(x3tm_ready, upto(b))
                nc.gpsimd.tensor_tensor(x3b[p][:, :, :], x3_tm[p][:, :, :], row_of(rows_sb[p], B_ROW), ALU.add).then_inc(x3b_ready, 1)

            def scale_n(X):
                b, p, n = X
                pool.wait_ge(ntm_ready, upto(b))
                nc.gpsimd.tensor_tensor(scaled[p][:, :, :], n_tm[p][:, :, :], row_of(rows_sb[p], G), ALU.mult).then_inc(scaled_ready, 1)

            def output(X):
                b, p, n = X
                pool.wait_ge(scaled_ready, upto(b))
                pool.wait_ge(x3b_ready, upto(b))
                if not isinstance(b, int) or b >= 2:
                    pool.wait_ge(stored[p], n * 16)
                nc.gpsimd.tensor_tensor(out_tm[p][:, :, :], scaled[p][:, :, :], x3b[p][:, :, :], ALU.add).then_inc(out_ready, 1)

            b0, b1_, b2 = HEAD
            choose_mask(b0, early=True)
            choose_mask(b1_, early=True)
            choose_mask(b2)

            def step(q, r):
                A, B, C, D, N = in_step(q, r)
                if D:
                    output_residual(D)
                    y_rstd(D)
                if N:
                    choose_mask(N)
                if D:
                    scale_n(D)
                    output(D)

            run(pool, step)
            t5, t6, t7 = TAIL
            output_residual(t5)
            y_rstd(t5)
            scale_n(t5)
            output(t5)
            output_residual(t6)
            y_rstd(t6)
            b, p, n = t6
            pool.wait_ge(first_n_ready, 1)
            g = rows_sb[p][:, G * DIM:(G + 1) * DIM]
            nc.gpsimd.tensor_tensor(scaled[p][:, 0, :], n_tm[p][:, 0, :], g, ALU.mult).then_inc(first_scaled_ready, 1)
            pool.wait_ge(first_scaled_ready, 1)
            pool.wait_ge(x3b_ready, upto(b))
            pool.wait_ge(stored[p], n * 16)
            nc.gpsimd.tensor_tensor(out_tm[p][:, 0, :], scaled[p][:, 0, :], x3b[p][:, 0, :], ALU.add).then_inc(out_ready, 1)
            y_rstd(t7)
            pool.wait_ge(ntm_ready, upto(b))
            nc.gpsimd.tensor_tensor(scaled[p][:, 1, :], n_tm[p][:, 1, :], g, ALU.mult).then_inc(scaled_ready, 1)


def kernel(x, itok_B_0_63, itok_B_0_2, itok_B_0_7, itok_B_0_6, L0_cond_W, L0_cond_b, L1_cond_W1, L1_cond_b1, L1_cond_v,
           L2_cond_weight, L2_cond_bias, L3_cond_down_w, L3_cond_down_b, L3_cond_up_w, L3_cond_up_b, L3_cond_ln_g, L3_cond_ln_b):
    import numpy as np
    import concourse.bacc as bacc
    from concourse.bass_utils import run_bass_kernel_spmd

    def rows(w):
        n, d, m = w.shape
        return w.reshape(n, d // P, P, m).transpose(0, 2, 1, 3).reshape(n, P, -1)

    a = {k: np.asarray(v) for k, v in dict(
        x=x, W0=L0_cond_W, b0=L0_cond_b, W1=L1_cond_W1, b1=L1_cond_b1, v=L1_cond_v, W2=L2_cond_weight, b2=L2_cond_bias,
        Wd=L3_cond_down_w, bd=L3_cond_down_b, Wu=L3_cond_up_w, bu=L3_cond_up_b, g=L3_cond_ln_g, b=L3_cond_ln_b).items()}
    host = {
        "xT": rows(a["x"].transpose(0, 2, 1)).reshape(BATCHES, P, CH, SEQ),
        "w0": np.concatenate([rows(a["W0"]), rows(a["b0"][:, :, None])], axis=2),
        "w1": rows(a["W1"][None]).reshape(P, CH, ATT),
        "b1": a["b1"].reshape(1, ATT),
        "v": a["v"].reshape(1, ATT),
        "w2": np.concatenate([rows(a["W2"].transpose(0, 2, 1)), rows(a["b2"][:, :, None])], axis=2),
        "w3": np.concatenate([rows(a["Wd"]), a["Wu"], a["bd"][:, :, None]], axis=2),
        "rows": np.concatenate([a["bu"], a["g"], a["b"]], axis=1),
        "ids": np.concatenate([np.asarray(i) for i in (itok_B_0_63, itok_B_0_2, itok_B_0_7, itok_B_0_6)]).reshape(1, 4 * BATCHES),
    }
    nc = bacc.Bacc("TRN2", target_bir_lowering=False, num_devices=1)
    arrays, args = {}, []
    for name, arr in host.items():
        arr = np.ascontiguousarray(arr)
        arrays[f"{name}_dram"] = arr
        args.append(nc.dram_tensor(f"{name}_dram", arr.shape, mybir.dt.from_np(arr.dtype), kind="ExternalInput").ap())
    args.append(nc.dram_tensor("out_dram", (BATCHES, P, TB, DIM), F32, kind="ExternalOutput").ap())
    build(nc, *args)
    r = run_bass_kernel_spmd(nc, [arrays], core_ids=[0])
    got = r.results[0]["out_dram"]
    return got.transpose(0, 2, 1, 3).reshape(BATCHES, SEQ, DIM)
```
